# Optimizing a Trainium2 kernel written in Bass

```python
import numpy as np
import jax
import jax.numpy as jnp

def _softmax(x, axis=-1):
    return jax.nn.softmax(x, axis=axis)

def _gelu(x):
    return jax.nn.gelu(x, approximate=True)

def _silu(x):
    return jax.nn.silu(x)

def _sigmoid(x):
    return jax.nn.sigmoid(x)

def _layernorm(x, axis=-1, eps=1e-05):
    m = jnp.mean(x, axis=axis, keepdims=True)
    v = jnp.var(x, axis=axis, keepdims=True)
    return (x - m) / jnp.sqrt(v + eps)

def _scatter_add(tgt, idx, src, axis=0):
    return tgt.at[idx].add(src)

def _segment_sum(src, seg, n):
    return jax.ops.segment_sum(src, seg, n)
kernel_name = 'mk_xattn_ffn_d2_seqx_r8_3bed34'

def setup_inputs(seed: int=0):
    np.random.seed(seed)
    _w = jnp.asarray

    def _rec_inputs():
        import jax
        import jax.numpy as jnp
        _rk = jax.random.key(seed)
        x = 7.22e-05 + 1 * jax.random.normal(jax.random.fold_in(_rk, 1), (8, 256, 128), jnp.float32)
        _lenS = 256 - jax.random.randint(jax.random.fold_in(_rk, 7), (8,), 0, max(1, 256 // 4) + 1, jnp.int32)
        _lenS2 = 256 - jax.random.randint(jax.random.fold_in(_rk, 8), (8,), 0, max(1, 256 // 4) + 1, jnp.int32)
        _ctx_1024P = jax.random.normal(jax.random.fold_in(_rk, 11), (8, 16, 128), jnp.float32)
        _ctx_1024c = jax.random.dirichlet(jax.random.fold_in(_rk, 511), 0.3 * jnp.ones((16,), jnp.float32), (8, 256))
        _ctx_1024t = jnp.einsum('bsk,bkd->bsd', _ctx_1024c, _ctx_1024P)
        _ctx_1024t = _ctx_1024t * jax.lax.rsqrt(jnp.mean(jnp.square(_ctx_1024t)) + 1e-12) * 0.953939
        ctx_1024 = 4.13588e-05 + 0.999923 * (_ctx_1024t + 0.3 * jax.random.normal(jax.random.fold_in(_rk, 611), (8, 256, 128), jnp.float32))
        return (x, ctx_1024)
    x, ctx_1024 = _rec_inputs()

    def _L0_xattn_setup():
        import jax, jax.numpy as jnp
        import numpy as np
        NUM_HEADS = 16
        key = jax.random.key(seed)
        k1, k2, k3, k4 = jax.random.split(key, 4)
        B, S, E = (4, 256, 128)
        return {'q': jax.random.normal(k1, (B, S, E), dtype=jnp.float32), 'k': jax.random.normal(k2, (B, S, E), dtype=jnp.float32), 'v': jax.random.normal(k3, (B, S, E), dtype=jnp.float32), 'w_out': jax.random.normal(k4, (E, E), dtype=jnp.float32) * E ** (-0.5), 'b_out': jnp.zeros((E,), dtype=jnp.float32)}
    _L0_xattn_all = _L0_xattn_setup()
    _L0_xattn_in = {k: v for k, v in _L0_xattn_all.items() if k in ('w_out', 'b_out')}
    del _L0_xattn_all

    def _L0_ffn_setup():
        import jax, jax.numpy as jnp
        import numpy as np
        D_MODEL = 128
        HIDDEN = 512
        N_EXPERTS = 8
        TOP_K = 2
        key = jax.random.key(seed)
        k_x, k_r, k_w1, k_w2 = jax.random.split(key, 4)
        x = jax.random.normal(k_x, (2, 128, D_MODEL), dtype=jnp.float32)
        Wr = jax.random.normal(k_r, (D_MODEL, N_EXPERTS), dtype=jnp.float32) * 0.02
        W1 = jax.random.normal(k_w1, (N_EXPERTS, D_MODEL, HIDDEN), dtype=jnp.float32) * 0.02
        W2 = jax.random.normal(k_w2, (N_EXPERTS, HIDDEN, D_MODEL), dtype=jnp.float32) * 0.02
        return {'x': x, 'Wr': Wr, 'W1': W1, 'W2': W2}
    _L0_ffn_all = _L0_ffn_setup()
    _L0_ffn_in = {k: v for k, v in _L0_ffn_all.items() if k in ('Wr', 'W1', 'W2')}
    del _L0_ffn_all

    def _L1_xattn_setup():
        import jax, jax.numpy as jnp
        import numpy as np
        D_MODEL = 128
        N_HEADS = 16
        D_K = D_MODEL // N_HEADS
        key = jax.random.key(seed)
        ks = jax.random.split(key, 11)
        B, L, S = (2, 256, 256)
        scale = 1.0 / np.sqrt(D_MODEL)
        return {'x_q': jax.random.normal(ks[0], (B, L, D_MODEL), jnp.float32), 'x_k': jax.random.normal(ks[1], (B, S, D_MODEL), jnp.float32), 'x_v': jax.random.normal(ks[2], (B, S, D_MODEL), jnp.float32), 'W_Q': jax.random.normal(ks[3], (D_MODEL, D_MODEL), jnp.float32) * scale, 'b_Q': jax.random.normal(ks[4], (D_MODEL,), jnp.float32) * 0.01, 'W_K': jax.random.normal(ks[5], (D_MODEL, D_MODEL), jnp.float32) * scale, 'b_K': jax.random.normal(ks[6], (D_MODEL,), jnp.float32) * 0.01, 'W_V': jax.random.normal(ks[7], (D_MODEL, D_MODEL), jnp.float32) * scale, 'b_V': jax.random.normal(ks[8], (D_MODEL,), jnp.float32) * 0.01, 'W_O': jax.random.normal(ks[9], (D_MODEL, D_MODEL), jnp.float32) * scale, 'b_O': jax.random.normal(ks[10], (D_MODEL,), jnp.float32) * 0.01}
    _L1_xattn_all = _L1_xattn_setup()
    _L1_xattn_in = {k: v for k, v in _L1_xattn_all.items() if k in ('W_Q', 'b_Q', 'W_K', 'b_K', 'W_V', 'b_V', 'W_O', 'b_O')}
    del _L1_xattn_all

    def _L1_ffn_setup():
        import jax, jax.numpy as jnp
        import numpy as np
        BLOCK = 32
        W_BITS = 4
        ACT_BITS = 16

        def act_qdq(x):
            qmax = 2.0 ** (ACT_BITS - 1) - 1.0
            scale = jnp.maximum(jnp.max(jnp.abs(x)) / qmax, 1e-12)
            return jnp.clip(jnp.round(x / scale), -qmax - 1.0, qmax) * scale

        def fixed_qdq_u16(x):
            scale = 1.0 / 65536.0
            return jnp.clip(jnp.round(x / scale), 0.0, 65535.0) * scale

        def lpbq_dequant(w):
            O, I = w.shape
            qmax = 2.0 ** (W_BITS - 1) - 1.0
            wb = w.reshape(O, I // BLOCK, BLOCK)
            s = jnp.maximum(jnp.max(jnp.abs(wb), axis=-1, keepdims=True) / qmax, 1e-12)
            wq = jnp.clip(jnp.round(wb / s), -qmax - 1.0, qmax) * s
            return wq.reshape(O, I)
        key = jax.random.key(seed)
        k1, k2, k3, k4 = jax.random.split(key, 4)
        B, S, H, I = (2, 512, 128, 384)
        x = jax.random.normal(k1, (B, S, H), jnp.float32)
        w_gate = jax.random.normal(k2, (I, H), jnp.float32) * 0.02
        w_up = jax.random.normal(k3, (I, H), jnp.float32) * 0.02
        w_down = jax.random.normal(k4, (H, I), jnp.float32) * 0.02
        return {'x': x, 'w_gate': w_gate, 'w_up': w_up, 'w_down': w_down}
    _L1_ffn_all = _L1_ffn_setup()
    _L1_ffn_in = {k: v for k, v in _L1_ffn_all.items() if k in ('w_gate', 'w_up', 'w_down')}
    del _L1_ffn_all
    return {'x': x, 'ctx_1024': ctx_1024, 'L0_xattn_w_out': _L0_xattn_in['w_out'], 'L0_xattn_b_out': _L0_xattn_in['b_out'], 'L0_ffn_Wr': _L0_ffn_in['Wr'], 'L0_ffn_W1': _L0_ffn_in['W1'], 'L0_ffn_W2': _L0_ffn_in['W2'], 'L1_xattn_W_Q': _L1_xattn_in['W_Q'], 'L1_xattn_b_Q': _L1_xattn_in['b_Q'], 'L1_xattn_W_K': _L1_xattn_in['W_K'], 'L1_xattn_b_K': _L1_xattn_in['b_K'], 'L1_xattn_W_V': _L1_xattn_in['W_V'], 'L1_xattn_b_V': _L1_xattn_in['b_V'], 'L1_xattn_W_O': _L1_xattn_in['W_O'], 'L1_xattn_b_O': _L1_xattn_in['b_O'], 'L1_ffn_w_gate': _L1_ffn_in['w_gate'], 'L1_ffn_w_up': _L1_ffn_in['w_up'], 'L1_ffn_w_down': _L1_ffn_in['w_down']}

def reference(x, ctx_1024, L0_xattn_w_out, L0_xattn_b_out, L0_ffn_Wr, L0_ffn_W1, L0_ffn_W2, L1_xattn_W_Q, L1_xattn_b_Q, L1_xattn_W_K, L1_xattn_b_K, L1_xattn_W_V, L1_xattn_b_V, L1_xattn_W_O, L1_xattn_b_O, L1_ffn_w_gate, L1_ffn_w_up, L1_ffn_w_down):
    import jax
    import jax.numpy as jnp

    def _L0_xattn_ref(q, k, v, w_out, b_out):
        import jax, jax.numpy as jnp
        import numpy as np
        NUM_HEADS = 16
        B, S, E = q.shape
        H = NUM_HEADS
        D = E // H
        scale = D ** (-0.5)

        def split(x):
            return x.reshape(B, S, H, D).transpose(0, 2, 1, 3)
        qh, kh, vh = (split(q), split(k), split(v))
        scores = jnp.einsum('bhqd,bhkd->bhqk', qh, kh) * scale
        weights = jax.nn.softmax(scores, axis=-1)
        out = jnp.einsum('bhqk,bhkd->bhqd', weights, vh)
        out = out.transpose(0, 2, 1, 3).reshape(B, S, E)
        return out @ w_out.T + b_out

    def _L0_ffn_ref(x, Wr, W1, W2):
        import jax, jax.numpy as jnp
        import numpy as np
        D_MODEL = 128
        HIDDEN = 512
        N_EXPERTS = 8
        TOP_K = 2
        B, S, D = x.shape
        flat = x.reshape(-1, D)
        logits = flat @ Wr
        top_vals, top_idx = jax.lax.top_k(logits, TOP_K)
        weights = jax.nn.softmax(top_vals, axis=-1)
        top1 = top_idx[:, 0]
        w_top1 = weights[:, 0]
        h = jax.nn.gelu(jnp.einsum('td,edh->teh', flat, W1), approximate=False)
        y = jnp.einsum('teh,ehd->ted', h, W2)
        y_sel = jnp.take_along_axis(y, top1[:, None, None], axis=1)[:, 0, :]
        out = (w_top1[:, None] * y_sel).reshape(B, S, D)
        return out

    def _L1_xattn_ref(x_q, x_k, x_v, W_Q, b_Q, W_K, b_K, W_V, b_V, W_O, b_O):
        import jax, jax.numpy as jnp
        import numpy as np
        D_MODEL = 128
        N_HEADS = 16
        D_K = D_MODEL // N_HEADS
        B, L, _ = x_q.shape
        S = x_k.shape[1]
        H, dk = (N_HEADS, D_K)
        Q = (x_q @ W_Q + b_Q).reshape(B, L, H, dk).transpose(0, 2, 1, 3)
        K = (x_k @ W_K + b_K).reshape(B, S, H, dk).transpose(0, 2, 1, 3)
        V = (x_v @ W_V + b_V).reshape(B, S, H, dk).transpose(0, 2, 1, 3)
        scores = jnp.einsum('bhld,bhsd->bhls', Q, K) / jnp.sqrt(jnp.float32(dk))
        attn = jax.nn.softmax(scores, axis=-1)
        ctx = jnp.einsum('bhls,bhsd->bhld', attn, V)
        ctx = ctx.transpose(0, 2, 1, 3).reshape(B, L, H * dk)
        out = ctx @ W_O + b_O
        return out

    def _L1_ffn_ref(x, w_gate, w_up, w_down):
        import jax, jax.numpy as jnp
        import numpy as np
        BLOCK = 32
        W_BITS = 4
        ACT_BITS = 16

        def act_qdq(x):
            qmax = 2.0 ** (ACT_BITS - 1) - 1.0
            scale = jnp.maximum(jnp.max(jnp.abs(x)) / qmax, 1e-12)
            return jnp.clip(jnp.round(x / scale), -qmax - 1.0, qmax) * scale

        def fixed_qdq_u16(x):
            scale = 1.0 / 65536.0
            return jnp.clip(jnp.round(x / scale), 0.0, 65535.0) * scale

        def lpbq_dequant(w):
            O, I = w.shape
            qmax = 2.0 ** (W_BITS - 1) - 1.0
            wb = w.reshape(O, I // BLOCK, BLOCK)
            s = jnp.maximum(jnp.max(jnp.abs(wb), axis=-1, keepdims=True) / qmax, 1e-12)
            wq = jnp.clip(jnp.round(wb / s), -qmax - 1.0, qmax) * s
            return wq.reshape(O, I)
        x = act_qdq(x)
        up = act_qdq(x @ lpbq_dequant(w_up).T)
        gate = act_qdq(x @ lpbq_dequant(w_gate).T)
        sig = fixed_qdq_u16(jax.nn.sigmoid(gate))
        gate = act_qdq(gate * sig)
        o = act_qdq(gate * up)
        return o @ lpbq_dequant(w_down).T
    x = x + _L0_xattn_ref(_layernorm(x, axis=-1), ctx_1024, ctx_1024, L0_xattn_w_out, L0_xattn_b_out)
    x = x + _L0_ffn_ref(_layernorm(x, axis=-1), L0_ffn_Wr, L0_ffn_W1, L0_ffn_W2)
    x = x + _L1_xattn_ref(_layernorm(x, axis=-1), ctx_1024, ctx_1024, L1_xattn_W_Q, L1_xattn_b_Q, L1_xattn_W_K, L1_xattn_b_K, L1_xattn_W_V, L1_xattn_b_V, L1_xattn_W_O, L1_xattn_b_O)
    x = x + _L1_ffn_ref(_layernorm(x, axis=-1), L1_ffn_w_gate, L1_ffn_w_up, L1_ffn_w_down)
    return x

_drawn_inputs = setup_inputs


def setup_inputs(seed=0):
    import zlib

    import numpy as np

    out = dict(_drawn_inputs(seed))
    spreads = {'L0_xattn_b_out': (0.0, 0.1)}
    factors = {'L0_ffn_Wr': 2.677,
     'L1_xattn_b_Q': 22.856,
     'L1_xattn_b_K': 64.0,
     'L1_xattn_b_V': 6.473,
     'L1_xattn_b_O': 6.422,
     'L1_ffn_w_gate': 6.896,
     'L1_ffn_w_up': 6.619,
     'L1_ffn_w_down': 6.648}
    for name, (base, spread) in spreads.items():
        noise = np.random.default_rng([zlib.crc32(name.encode()), seed]).standard_normal(out[name].shape)
        drawn = base * np.exp(spread * noise) if base else spread * noise
        out[name] = jnp.asarray(drawn.astype(out[name].dtype))
    for name, factor in factors.items():
        out[name] = (out[name] * factor).astype(out[name].dtype)
    return out
```

```python
from contextlib import ExitStack

import concourse.bass as bass
from concourse import mybir

ALU = mybir.AluOpType
ACT = mybir.ActivationFunctionType
AX = mybir.AxisListType
F32 = mybir.dt.float32
BF16 = mybir.dt.bfloat16
I32 = mybir.dt.int32
I16 = mybir.dt.int16
U16 = mybir.dt.uint16

P = 128
B, S, D = 8, 256, 128
H, DK = 16, 8
NT = B * S // P
TPB = S // P
PAIRS = H // 2
QUADS = H // 4
E8 = 8
HID = 512
HC = HID // P
REG = B * S + P
MT = NT + E8 - 1
FF = 384
FC = FF // P
BLK = 32
EPS = 1e-5
ACT_QMAX = 2.0 ** 15 - 1.0
W_QMAX = 2.0 ** 3 - 1.0
TINY = 1e-12
Q_SLOT = (0, 0, 0, 1, 1, 2)
K_SLOT = (0, 1, 2, 0, 1, 0)
SLOTS = len(Q_SLOT)
SROWS = SLOTS * DK
MROW = P - 2 * 3
RING = 4
ISQ = float(DK) ** -0.5
MAGIC = 1.5 * 2.0 ** 23
NB = FC * B * S // 512


def emit(nc, A, out):
    ctx = ExitStack()
    with ctx:
        def sb(name, shape, dt=F32):
            return ctx.enter_context(nc.sbuf_tensor(name, shape, dt))

        sems = {}

        def sm(name, i=""):
            key = f"{name}_{i}"
            if key not in sems:
                sems[key] = ctx.enter_context(nc.semaphore(key))
            return sems[key]

        PER_LAYER = dict(st_done=8 * B, exp_done=8 * B, a_done=16 * B, red_done=16 * B, pv_done=4 * B, 
                         parts_ready=B, q_evac=2 * B, mt_evac=B, mt_done=B, mx_ready=B, v_ready=B, xn_ready=B, 
                         xn2_ready=B, t_done=B, ot_evac=B, ont_done=B, ont_evac=B, ott_done=B, norm_done=B, 
                         y_done=B, x_done=B, guess=15, ln_done=15, bn=15, aggr=15, ve=15, half=15, 
                         q_loaded=16 * 12 * (B // RING), m_loaded=16 * 2 * (B // 2))

        def upto(name, L, n, i=""):
            return sm(name, i), n + L * PER_LAYER[name]

        T, V, G, C = nc.tensor, nc.vector, nc.gpsimd, nc.scalar

        ident = sb("ident", [P, P])
        identb = sb("identb", [P, P], BF16)
        ones = sb("ones", [P, P])
        before = sb("before", [P, P])
        x = sb("x", [P, NT, D])
        xn = sb("xn", [P, NT, D])
        ctxt = sb("ctxt", [P, NT, D])
        v1 = sb("v1", [P, NT, D])
        kstack = sb("kstack", [P, RING, 2, PAIRS, S], BF16)
        qstack = sb("qstack", [P, RING, PAIRS, S], BF16)
        qparts = sb("qparts", [P, 2, 3, S], BF16)
        qf = sb("qf", [P, 2, S])
        qr = sb("qr", [P, S])
        xnt = sb("xnt", [P, S])
        ex = sb("ex", [P, 4, 2, TPB, S])
        vpad = sb("vpad", [P, 2, TPB, H, 32])
        mx = sb("mx", [P, 2, TPB, 2, PAIRS])
        mr = sb("mr", [P, TPB, 2, PAIRS])
        mparts = sb("mparts", [P, TPB, 2, 3, PAIRS], BF16)
        mt = sb("mt", [2 * 3 * PAIRS, 2, S], BF16)
        ot = sb("ot", [P, 2, S])
        rec = sb("rec", [P, TPB, H])
        on = sb("on", [P, TPB, D])
        ont = sb("ont", [P, S])
        xsb = ot[:, :, :].rearrange("p a (b d) -> p (a b) d", b=2)
        xst = ont[:, :].rearrange("p (a t) -> p a t", a=2)
        ysb = on
        wo = [sb("wo0", [P, D]), sb("wo1", [P, D])]
        bo = [sb("bo0", [P, D]), sb("bo1", [P, D])]
        wq = sb("wq", [P, D])
        wk = sb("wk", [P, D])
        wv = sb("wv", [P, D])
        bv = sb("bv", [P, D])
        bqk = sb("bqk", [P, 2])
        stat = sb("stat", [P, 2, 4, 6])
        mv = sb("mv", [P, 2, 4, 2])
        nw = sb("nw", [P, 2, 3, 4])
        nmr = sb("nmr", [P, 2, 4])
        w12 = sb("w12", [P, E8 * 2 * HID])
        c28 = sb("c28", [P, 7168])
        ctx_t = c28[:, 0:2048]
        kr = c28[:, 2048:4096]
        kp = c28[:, 4096:7168].bitcast(BF16).rearrange("p (c t) -> p c t", c=3)
        t2 = sb("t2", [P, S])
        wr = sb("wr", [P, E8])
        epri = sb("epri", [P, E8])
        tidx = sb("tidx", [P, MT])
        lg = sb("lg", [P, NT, E8])
        v8 = sb("v8", [P, NT, E8])
        oh = sb("oh", [P, NT, E8])
        run = sb("run", [P, NT + 1, E8])
        tmp = sb("tmp", [P, NT, E8])
        m1 = sb("m1", [P, NT])
        posf = sb("posf", [P, NT])
        ebase = sb("ebase", [P, NT])
        gate = sb("gate", [P, NT])
        ntile = sb("ntile", [P, E8])
        ntile_i = sb("ntile_i", [P, E8], I16)
        cnt = sb("cnt", [P, E8])
        cnt_i = sb("cnt_i", [P, E8], I32)
        incl = sb("incl", [P, E8])
        excl = sb("excl", [P, E8])
        slot = sb("slot", [P, NT], I32)
        gslot = sb("gslot", [P, NT], I32)
        cmp_ = sb("cmp_", [P, MT, E8])
        texpf = sb("texpf", [P, MT])
        toff = sb("toff", [P, MT])
        texp = sb("texp", [P, MT], I32)
        tbase = sb("tbase", [P, MT], I32)
        zt = sb("zt", [P, D])
        hg = sb("hg", [P, 2, HID])
        w3 = sb("w3", [P, 3 * FF])
        w3t = sb("w3t", [P, 3 * FF])
        w3i = sb("w3i", [P, 3 * FF], I16)
        wam = sb("wam", [P, 3 * FF // BLK])
        wrs = sb("wrs", [P, 3 * FF // BLK])
        sc = sb("sc", [P, 64])
        am = sb("am", [P, 5, NB])
        magic = sb("magic", [P, 1])
        ex_flat = ex[:, :, :, :, :].rearrange("p a b c d -> p (a b c d)")
        kst_f = kstack[:, :, :, :, :].rearrange("p a b c d -> p (a b c d)").bitcast(F32)
        qst_f = qstack[:, :, :, :].rearrange("p a b c -> p (a b c)").bitcast(F32)

        kd = [nc.dram_tensor(f"kd{i}", (2, SROWS, PAIRS, B * S), BF16, kind="Internal").ap() for i in range(2)]
        xs_d = nc.dram_tensor("xs_d", (E8 * REG + P, D), F32, kind="Internal").ap()
        ys_d = nc.dram_tensor("ys_d", (MT * P, D), F32, kind="Internal").ap()

        ps = [ctx.enter_context(nc.psum_tensor(f"ps{i}", [P, 512], F32)) for i in range(8)]
        st_bank = [[ps[0], ps[1]], [ps[2], ps[3]]]
        a_bank = [ps[4], ps[5]]
        o_bank, misc = ps[6], ps[7]

        x_v = A["x"].rearrange("b (t p) d -> p (b t) d", p=P)
        c_v = A["ctx_1024"].rearrange("b (t p) d -> p (b t) d", p=P)

        chains = {}

        def link(eng, ins, name):
            chains[name] = chains.get(name, 0) + 1
            ins.then_inc(sm(name), 1)
            eng.wait_ge(sm(name), chains[name])

        def perm(ap):
            return ap.rearrange("a (p r d) -> a r d p", r=2, d=DK)

        def as_perm(ap):
            return ap.rearrange("a (r d p) -> a r d p", r=2, d=DK)

        def flat(ap):
            return ap.rearrange("p a b -> p (a b)")

        def keys0_pe(pe):
            pe.wait_ge(sm("ident"), 1)
            for c in range(4):
                pe.wait_ge(sm("cperm"), 4 * c + 4)
                for t in range(4):
                    last = T.transpose(ps[c][:, P * t:P * t + P], xn[:, 4 * c + t, :], ident[:, :])
                last.then_inc(sm("p_k", 0), 1)

        def keys1_pe(pe):
            pe.wait_ge(*upto("exp_done", 0, 8 * B))
            for c in range(4):
                for t in range(4):
                    last = T.transpose(ps[c][:, P * t:P * t + P], ctxt[:, 4 * c + t, :], ident[:, :])
                last.then_inc(sm("p_ct"), 1)
            pe.wait_ge(sm("ld_w"), 16 * 12)
            for c in range(4):
                pe.wait_ge(sm("a_ct"), c + 1)
                T.matmul(ps[c][:, :], wk[:, :], ctx_t[:, 512 * c:512 * c + 512], start=True, stop=True).then_inc(sm("p_k", 1), 1)

        def keys1_act(act):
            for c in range(4):
                act.wait_ge(sm("p_ct"), c + 1)
                C.copy(ctx_t[:, 512 * c:512 * c + 512], ps[c][:, :]).then_inc(sm("a_ct"), 1)
            act.wait_ge(sm("ld_w"), 16 * 12)
            act.wait_ge(sm("kd_stored", 0), 192)
            for c in range(4):
                act.wait_ge(sm("p_k", 1), c + 1)
                C.activation(kp[:, 0, 512 * c:512 * c + 512], ps[c][:, :], ACT.Identity, bias=bqk[:, 1:2]).then_inc(sm("a_k", 1), 1)

        def keys_dve(dve, L, c):
            col = slice(512 * c, 512 * c + 512)
            dve.wait_ge(sm("a_k", L), c + 1)
            if L == 0:
                link(dve, V.tensor_tensor(kr[:, col], ps[c][:, :], kp[:, 0, col], ALU.subtract), "dve_chain")
            else:
                link(dve, V.scalar_tensor_tensor(kr[:, col], ps[c][:, :], bqk[:, 1:2], kp[:, 0, col], ALU.add, ALU.subtract), "dve_chain")
            link(dve, V.tensor_copy(kp[:, 1, col], kr[:, col]), "dve_chain")
            V.tensor_tensor(kp[:, 2, col], kr[:, col], kp[:, 1, col], ALU.subtract).then_inc(sm("d_k", L), 1)

        def keys_sp(sp, L):
            sp.wait_ge(sm("a_k", L), 4)
            sp.wait_ge(sm("d_k", L), 4)
            for s, c in enumerate(K_SLOT):
                for r in range(2):
                    sp.dma_start(kd[L][r, DK * s:DK * s + DK].rearrange("d p t -> (d p) t"), kp[64 * r:64 * r + 64, c, :]).then_inc(sm("kd_stored", L), 16)

        def values1_pe(pe, c):
            pe.wait_ge(sm("d_k", 1), c + 1)
            for t in range(4):
                k = P * (4 * c + t)
                last = T.matmul(ps[c][:, P * t:P * t + P], ctx_t[:, k:k + P], wv[:, :], start=(t == 0), stop=(t == 3), skip_group_check=True)
            last.then_inc(sm("p_v1"), 1)

        def values1_dve(dve, c):
            dve.wait_ge(sm("p_v1"), c + 1)
            V.tensor_tensor(v1[:, 4 * c:4 * c + 4, :], ps[c][:, :].rearrange("p (t d) -> p t d", t=4),
                            bv[:, :].unsqueeze(1).to_broadcast([P, 4, D]), ALU.add).then_inc(sm("d_v1"), 1)

        def prologue_sp(sp):
            for i in range(4):
                sp.dma_start(ctxt[:, 4 * i:4 * i + 4, :], c_v[:, 4 * i:4 * i + 4, :]).then_inc(sm("ld_ctx", i), 16)
            sp.wait_ge(sm("kzero"), 4)
            sp.wait_ge(sm("qzero"), 2)
            sp.wait_ge(sm("d_k", 0), 1)
            for r in range(2):
                for s, c in enumerate(K_SLOT):
                    k = SROWS * r + DK * s
                    sp.dma_start(kstack[k:k + DK, 0, r, :, :], kp[64 * r:64 * r + 64, c, 0:S]).then_inc(sm("k_first"), 16)
            sp.wait_ge(sm("neg"), 1)
            for i in range(RING):
                for r in range(2):
                    k = MROW + 3 * r
                    sp.dma_start(kstack[k:k + 3, i, r, :, :], mt[0:3 * PAIRS, 0, :]).then_inc(sm("neg_stored"), 16)

        def prologue_act(act):
            act.dma_start(x[:, 0:4, :], x_v[:, 0:4, :]).then_inc(sm("ld_x", 0), 16)
            act.dma_start(x[:, 4:16, :], x_v[:, 4:16, :]).then_inc(sm("ld_x", 1), 16)
            with nc.allow_non_contiguous_dma(reason="two vectors of 128 elements"):
                for i, n in enumerate(("b_q", "b_k")):
                    act.dma_start(bqk[:, i:i + 1], A[n].unsqueeze(1)).then_inc(sm("ld_w"), 16)
            for dst, n in ((wq, "w_q"), (wk, "w_k"), (wv, "L1_xattn_W_V"), (wo[0], "w_out_t"), (wo[1], "L1_xattn_W_O"), (wr, "L0_ffn_Wr")):
                act.dma_start(dst[:, :], A[n]).then_inc(sm("ld_w"), 16)
            for dst, n in ((bo[0], "L0_xattn_b_out"), (bo[1], "L1_xattn_b_O"), (bv, "L1_xattn_b_V")):
                act.dma_start(dst[:, :], A[n].partition_broadcast(P)).then_inc(sm("ld_w"), 16)
            act.dma_start(w3[:, 2 * FF:3 * FF], A["L1_ffn_w_down"]).then_inc(sm("ld_w"), 16)
            for c in range(4):
                act.wait_ge(sm("p_k", 0), c + 1)
                C.copy(kp[:, 0, 512 * c:512 * c + 512], ps[c][:, :]).then_inc(sm("a_k", 0), 1)

        def prologue_pool(pool):
            G.memset(ident[:, :], 0.0).then_inc(sm("pool_chain"), 1)
            chains["pool_chain"] = 1
            pool.wait_ge(sm("pool_chain"), 1)
            G.affine_select(out=ident[:, :], in_=ident[:, :], compare_op=ALU.not_equal, fill=1.0, base=0,
                            pattern=[[-1, P]], channel_multiplier=1).then_inc(sm("ident"), 1)
            for i in (2, 3):
                G.memset(kst_f[:, 2048 * i:2048 * i + 2048], 0.0).then_inc(sm("kzero"), 1)
            for i in range(2):
                G.memset(qst_f[:, 2048 * i:2048 * i + 2048], 0.0).then_inc(sm("qzero"), 1)
            G.memset(ones[:, :], 1.0).then_inc(sm("consts"), 1)
            G.memset(zt[:, :], 0.0).then_inc(sm("consts"), 1)
            G.memset(run[:, 0, :], 0.0).then_inc(sm("consts"), 1)
            G.iota(epri[:, :], [[-1, E8]], base=E8, channel_multiplier=0, allow_small_or_imprecise_dtypes=True).then_inc(sm("consts"), 1)
            G.iota(tidx[:, :], [[1, MT]], base=0, channel_multiplier=0, allow_small_or_imprecise_dtypes=True).then_inc(sm("consts"), 1)
            pool.wait_ge(sm("ident"), 1)
            G.tensor_copy(identb[:, :], ident[:, :]).then_inc(sm("consts"), 1)
            pool.wait_ge(sm("consts"), 6)
            G.affine_select(out=before[:, :], in_=ones[:, :], compare_op=ALU.is_gt, fill=0.0, base=0, pattern=[[1, P]],
                            channel_multiplier=-1).then_inc(sm("consts"), 1)

        def prologue_pool_late(pool):
            link(pool, G.memset(vpad[:, :, :, :, :], 0.0), "pool_chain")
            for q in range(QUADS):
                o = 9 * (q % 3) + DK
                last = G.memset(vpad[:, :, :, 4 * q:4 * q + 4, o:o + 1], 1.0)
            link(pool, last, "pool_chain")

        def prologue_dve(dve):
            V.memset(mt[:, :, :], -1.0).then_inc(sm("neg"), 1)
            for i in (0, 1):
                V.memset(kst_f[:, 2048 * i:2048 * i + 2048], 0.0).then_inc(sm("kzero"), 1)
            V.memset(magic[:, :], MAGIC)
            for t in range(NT):
                if t % 4 == 0:
                    dve.wait_ge(sm("ld_ctx", t // 4), 16)
                V.tensor_copy(as_perm(xn[:, t, :]), perm(ctxt[:, t, :])).then_inc(sm("cperm"), 1)
                if t == 3:
                    dve.wait_ge(sm("ld_x", 0), 16)
            keys_dve(dve, 0, 0)

        def prologue_dve_late(dve, c):
            keys_dve(dve, 0, c)

        first_b, last_b = -6, B + 5
        steps = [(b, s) for b in range(first_b, last_b) for s in range(8)]
        LNB = -5

        def ok(b):
            return 0 <= b < B

        def scores_at(b, s):
            g = 8 * b + s + 12
            return g // 8, g % 8

        def ln_cols(b):
            return (0 if ok(b + 5) else 2), (4 if ok(b - 2) else 2)

        def attention_sp(sp, L):
            for b, s in steps:
                if L == 0 and (b, s) == (-3, 1):
                    keys_sp(sp, 0)
                    sp.dma_start(w12[:, :].rearrange("p (e n) -> p e n", e=E8)[:, :, 0:HID], A["L0_ffn_W1"].rearrange("e d h -> d e h")).then_inc(sm("ld_e"), 16)
                    for e in range(E8):
                        o = 2 * HID * e + HID
                        sp.dma_start(w12[:, o:o + HID].rearrange("p (c d) -> p c d", c=HC), A["L0_ffn_W2"][e].rearrange("(c p) d -> p c d", p=P)).then_inc(sm("ld_e"), 16)
                    for i, n in enumerate(("L1_ffn_w_gate", "L1_ffn_w_up")):
                        sp.dma_start(w3[:, FF * i:FF * i + FF].rearrange("p (c h) -> p c h", c=FC), A[n].rearrange("(c p) h -> p c h", p=P)).then_inc(sm("ld_e"), 16)
                if s == 0 and ok(b + 3):
                    n = b + 3
                    if n >= RING:
                        sp.wait_ge(*upto("st_done", L, 8 * (n - RING) + 8))
                    if L == 1 and n == 0:
                        sp.wait_ge(*upto("st_done", 0, 8 * B))
                    if L == 1 or n > 0:
                        sp.wait_ge(sm("kd_stored", L), 192)
                        for r in range(2):
                            sp.dma_start(kstack[SROWS * r:SROWS * r + SROWS, n % RING, r, :, :], kd[L][r, :, :, S * n:S * n + S]).then_inc(sm(f"k_loaded{L}", n % RING), 16)
                    sp.wait_ge(*upto("parts_ready", L, n + 1))
                    for r in range(2):
                        for i, c in enumerate(Q_SLOT):
                            k = SROWS * r + DK * i
                            sp.dma_start(qstack[k:k + DK, n % RING, :, :], qparts[64 * r:64 * r + 64, n % 2, c, :]).then_inc(sm("q_loaded", n % RING), 16)
                if s == 6 and ok(b + 1):
                    n = b + 1
                    sp.wait_ge(*upto("mt_evac", L, n + 1))
                    for r in range(2):
                        k = MROW + 3 * r
                        sp.dma_start(qstack[k:k + 3, n % RING, :, :], mt[24 * r:24 * r + 24, n % 2, :]).then_inc(sm("m_loaded", n % 2), 16)

        def attention_pool(pool, L):
            vsrc = ctxt if L == 0 else v1

            def pl(ins):
                link(pool, ins, "pool_chain")
            for b, s in steps:
                if s == 0 and ok(b + 3):
                    n = b + 3
                    pool.wait_ge(*upto("q_evac", L, 2 * n + 2))
                    if n >= 2:
                        pool.wait_ge(*upto("q_loaded", L, 192 * ((n - 2) // RING + 1), (n - 2) % RING))
                    pl(G.tensor_tensor(qr[:, :], qf[:, n % 2, :], qparts[:, n % 2, 0, :], ALU.subtract))
                    pl(G.tensor_scalar(qparts[:, n % 2, 1, :], qr[:, :], 1.0, None, ALU.mult))
                    G.tensor_tensor(qparts[:, n % 2, 2, :], qr[:, :], qparts[:, n % 2, 1, :], ALU.subtract).then_inc(sm("parts_ready"), 1)
                if L == 0 and s == 1 and ok(b - 4):
                    n = b - 4
                    t = slice(2 * n, 2 * n + 2)
                    pool.wait_ge(sm("pos_red"), n + 1)
                    pl(G.tensor_scalar(ebase[:, t], m1[:, t], -float(REG), float(E8 * REG), ALU.mult, ALU.add))
                    pl(G.tensor_tensor(ebase[:, t], posf[:, t], ebase[:, t], ALU.add))
                    pl(G.tensor_copy(slot[:, t], ebase[:, t]))
                    for k in (2 * n, 2 * n + 1):
                        G.indirect_dma_start(out=xs_d, out_offset=bass.IndirectOffsetOnAxis(ap=slot[:, k:k + 1], axis=0),
                                             in_=xn[:, k, :], in_offset=None).then_inc(sm("scattered"), 16)
                if s == 2 and ok(b + 4):
                    n = b + 4
                    k = (b - 1) % 2
                    if L == 0 and n < 4:
                        pool.wait_ge(sm("p_k", 0), (2 * n + 1) // 4 + 1)
                    for i in range(2):
                        t = 2 * n + i
                        dst = xn[:, t, :]
                        last = G.tensor_scalar(as_perm(dst) if L == 0 else dst, perm(x[:, t, :]) if L == 0 else x[:, t, :],
                                               nw[:, k, 1, i:i + 1], nmr[:, k, i:i + 1], ALU.mult, ALU.add)
                    pl(last)
                    if L == 0 and n == 0:
                        pool.wait_ge(sm("ld_w"), 16 * 12)
                    G.tensor_tensor(x[:, 2 * n:2 * n + 2, :], x[:, 2 * n:2 * n + 2, :],
                                    bo[L][:, :].unsqueeze(1).to_broadcast([P, 2, D]), ALU.add).then_inc(sm("xn_ready"), 1)
                    if L == 0 and n == 0:
                        prologue_pool_late(pool)
                if s == 3 and ok(b + 1):
                    n = b + 1
                    if n >= 2:
                        pool.wait_ge(*upto("pv_done", L, 4 * (n - 2) + 4))
                    elif L == 0:
                        pool.wait_ge(sm("ld_ctx", 0), 16)
                    else:
                        pool.wait_ge(*upto("pv_done", 0, 4 * B))
                        pool.wait_ge(sm("d_v1"), 4)
                    if L == 0 and n % 2 == 0:
                        pool.wait_ge(sm("ld_ctx", n // 2), 16)
                    for q in range(QUADS):
                        o = 9 * (q % 3)
                        last = G.tensor_copy(vpad[:, n % 2, :, 4 * q:4 * q + 4, o:o + DK],
                                             vsrc[:, 2 * n:2 * n + 2, 32 * q:32 * q + 32].rearrange("p t (j d) -> p t j d", j=4))
                    last.then_inc(sm("v_ready"), 1)
                if s == 4 and ok(b + 1):
                    n = b + 1
                    pool.wait_ge(*upto("red_done", L, 16 * n + 16))
                    if n >= 1:
                        pool.wait_ge(*upto("mt_done", L, n))
                    m_, r_ = mx[:, n % 2], mr[:, :, :, :]
                    pl(G.tensor_scalar(mparts[:, :, :, 0, :], m_, 1.0, None, ALU.mult))
                    pl(G.tensor_tensor(r_, m_, mparts[:, :, :, 0, :], ALU.subtract))
                    pl(G.tensor_scalar(mparts[:, :, :, 1, :], r_, 1.0, None, ALU.mult))
                    G.tensor_tensor(mparts[:, :, :, 2, :], r_, mparts[:, :, :, 1, :], ALU.subtract).then_inc(sm("mx_ready"), 1)
                if s == 5 and (ok(b + 5) or ok(b - 2)):
                    pool.wait_ge(*upto("guess", L, b - LNB + 1))
                    c = slice(*ln_cols(b))
                    ve, y, a = (nw[:, b % 2, i, c] for i in range(3))
                    for i in range(3):
                        pl(G.tensor_tensor(a, y, y, ALU.mult))
                        pl(G.tensor_tensor(a, a, ve, ALU.mult))
                        pl(G.tensor_scalar(a, a, -0.5, 1.5, ALU.mult, ALU.add))
                        pl(G.tensor_tensor(y, y, a, ALU.mult))
                    pl(G.tensor_tensor(a, mv[:, b % 2, c, 0], y, ALU.mult))
                    last = G.tensor_scalar(nmr[:, b % 2, c], a, -1.0, None, ALU.mult)
                    last.then_inc(sm("ln_done"), 1)
                    pool.wait_ge(*upto("ln_done", L, b - LNB + 1))
                if L == 0 and s == 5 and ok(b - 3):
                    n = b - 3
                    pool.wait_ge(sm("oh_done"), n + 1)
                    pl(G.tensor_tensor(run[:, 2 * n + 1, :], run[:, 2 * n, :], oh[:, 2 * n, :], ALU.add))
                    G.tensor_tensor(run[:, 2 * n + 2, :], run[:, 2 * n + 1, :], oh[:, 2 * n + 1, :], ALU.add).then_inc(sm("run_done"), 1)
                    pool.wait_ge(sm("run_done"), n + 1)
                if L == 1 and s == 6 and ok(b + 6):
                    for t in (2 * b + 12, 2 * b + 13):
                        G.indirect_dma_start(out=ctxt[:, t, :], out_offset=None, in_=ys_d,
                                             in_offset=bass.IndirectOffsetOnAxis(ap=gslot[:, t:t + 1], axis=0)).then_inc(sm("gathered", b + 6), 16)
                if s == 7 and ok(b - 2):
                    n = b - 2
                    for i in range(2):
                        t = 2 * n + i
                        last = G.tensor_scalar(xn[:, t, :], x[:, t, :], nw[:, b % 2, 1, 2 + i:3 + i], nmr[:, b % 2, 2 + i:3 + i], ALU.mult, ALU.add)
                    last.then_inc(sm("xn2_ready"), 1)
                    pool.wait_ge(*upto("xn2_ready", L, n + 1))

        def attention_act(act, L):
            for b, s in steps:
                if ok(b):
                    n = 8 * b + s
                    act.wait_ge(*upto("st_done", L, n + 1))
                    if n >= 4:
                        act.wait_ge(*upto("pv_done", L, (n - 4) // 2 + 1))
                    for r in range(2):
                        last = C.activation(ex[:, n % 4, r, :, :], st_bank[n % 2][r][:, :].rearrange("p (k q) -> p k q", k=2), ACT.Exp, scale=ISQ)
                    last.then_inc(sm("exp_done"), 1)
                if s == 6 and ok(b + 4):
                    n = b + 4
                    act.wait_ge(*upto("t_done", L, n + 1))
                    if L == 0:
                        if n >= 2:
                            act.wait_ge(*upto("parts_ready", L, n - 1))
                            act.wait_ge(*upto("q_loaded", L, 192 * ((n - 2) // RING + 1), (n - 2) % RING))
                        C.copy(qf[:, n % 2, :], misc[:, 0:S]).then_inc(sm("q_evac"), 1)
                        C.copy(qparts[:, n % 2, 0, :], misc[:, 0:S]).then_inc(sm("q_evac"), 1)
                    else:
                        C.copy(xnt[:, :], misc[:, 0:S]).then_inc(sm("xnt_evac"), 1)
                if L == 1 and s == 7 and ok(b + 4):
                    n = b + 4
                    act.wait_ge(sm("qp_done"), n + 1)
                    if n >= 2:
                        act.wait_ge(*upto("parts_ready", L, n - 1))
                        act.wait_ge(*upto("q_loaded", L, 192 * ((n - 2) // RING + 1), (n - 2) % RING))
                    C.activation(qf[:, n % 2, :], misc[:, 0:S], ACT.Identity, bias=bqk[:, 0:1]).then_inc(sm("q_evac"), 1)
                    C.activation(qparts[:, n % 2, 0, :], misc[:, 0:S], ACT.Identity, bias=bqk[:, 0:1]).then_inc(sm("q_evac"), 1)
                if L == 0 and (b, s) == (B, 5):
                    keys1_act(act)
                if L == 0 and s == 0 and ok(b - 3):
                    act.wait_ge(sm("t2_done"), b - 2)
                    C.copy(t2[:, :], misc[:, 0:S]).then_inc(sm("t2_evac"), 1)
                if L == 0 and s == 1 and ok(b - 3):
                    n = b - 3
                    act.wait_ge(sm("lg_done"), n + 1)
                    C.copy(lg[:, 2 * n:2 * n + 2, :], misc[:, 0:2 * E8].rearrange("p (t e) -> p t e", t=2)).then_inc(sm("lg_evac"), 1)
                if s == 1 and ok(b - 1):
                    act.wait_ge(*upto("pv_done", L, 4 * b))
                    if b >= 2:
                        act.wait_ge(*upto("ott_done", L, b - 1))
                    C.copy(ot[:, :, :], o_bank[:, :].rearrange("p (a q) -> p a q", a=2)).then_inc(sm("ot_evac"), 1)
                if s == 3 and ok(b - 1):
                    act.wait_ge(*upto("ont_done", L, b))
                    C.copy(ont[:, :], misc[:, 0:S]).then_inc(sm("ont_evac"), 1)
                if s == 5 and ok(b + 1):
                    n = b + 1
                    act.wait_ge(*upto("mt_done", L, n + 1))
                    if n >= 2:
                        act.wait_ge(*upto("m_loaded", L, 32 * (n // 2), n % 2))
                    if L == 0 and n == 0:
                        act.wait_ge(sm("neg_stored"), 16 * 2 * RING)
                    C.copy(mt[:, n % 2, :], misc[0:48, 0:S]).then_inc(sm("mt_evac"), 1)

        def attention_dve(dve, L):
            def dl(ins):
                link(dve, ins, "dve_chain")
            for b, s in steps:
                def small_steps():
                    if ok(b + 5) or ok(b - 2):
                        c0, c1 = ln_cols(b)
                        c = slice(c0, c1)
                        ve, y, a = (nw[:, b % 2, i, c] for i in range(3))
                        if s == 0:
                            if b - 2 >= LNB:
                                dve.wait_ge(*upto("ln_done", L, b - 2 - LNB + 1))
                            for i in range(c0, c1):
                                t = 2 * (b + 5) + i if i < 2 else 2 * (b - 2) + i - 2
                                if i == 0 and L == 0:
                                    dve.wait_ge(sm("ld_x", 0 if b + 5 < 2 else 1), 16)
                                if i == 2:
                                    dve.wait_ge(*upto("x_done", L, b - 1))
                                if i == 0 and L == 1:
                                    dve.wait_ge(sm("combined"), b + 6)
                                last = V.bn_stats(stat[:, b % 2, i, :], x[:, t, :])
                            last.then_inc(sm("bn"), 1)
                        if s == 1:
                            dve.wait_ge(*upto("bn", L, b - LNB + 1))
                            for i in range(c0, c1):
                                last = V.bn_aggr(mv[:, b % 2, i, :], stat[:, b % 2, i, :])
                            last.then_inc(sm("aggr"), 1)
                        if s == 2:
                            dve.wait_ge(*upto("aggr", L, b - LNB + 1))
                            V.tensor_scalar(ve, mv[:, b % 2, c, 1], EPS, None, ALU.add).then_inc(sm("ve"), 1)
                        if s == 3:
                            dve.wait_ge(*upto("ve", L, b - LNB + 1))
                            V.tensor_scalar(a.bitcast(I32), ve.bitcast(I32), 1, None, ALU.logical_shift_right).then_inc(sm("half"), 1)
                        if s == 4:
                            dve.wait_ge(*upto("half", L, b - LNB + 1))
                            if ok(b + 3):
                                dve.wait_ge(*upto("xn_ready", L, b + 4))
                            if ok(b - 4):
                                dve.wait_ge(*upto("xn2_ready", L, b - 3))
                            V.tensor_scalar(y.bitcast(I32), a.bitcast(I32), -1.0, float(0x5F3759DF), ALU.mult, ALU.add).then_inc(sm("guess"), 1)

                n, p = scores_at(b, s)
                if L == 1 and s == 7 and ok(b + 6):
                    m = b + 6
                    dve.wait_ge(sm("gathered", m), 32)
                    for t in (2 * m, 2 * m + 1):
                        last = V.scalar_tensor_tensor(x[:, t, :], ctxt[:, t, :], gate[:, t:t + 1], x[:, t, :], ALU.mult, ALU.add)
                    last.then_inc(sm("combined"), 1)
                for r in range(2):
                    if ok(n):
                        u = 16 * n + 2 * p + r
                        dve.wait_ge(*upto("a_done", L, u + 1))
                        if n >= 2:
                            dve.wait_ge(*upto("mx_ready", L, n - 1))
                        V.reduce_max(mx[:, n % 2, :, r, p], a_bank[r][:, :].rearrange("q (t k) -> q t k", t=2), AX.X).then_inc(sm("red_done"), 1)
                    if r == 0:
                        small_steps()
                if L == 0 and b == -4 and 1 <= s <= 3:
                    prologue_dve_late(dve, s)
                if L == 0 and s == 1 and ok(b - 3):
                    m = b - 3
                    dve.wait_ge(sm("lg_evac"), m + 1)
                    for t in (2 * m, 2 * m + 1):
                        last = V.max(v8[:, t, :], lg[:, t, :])
                    last.then_inc(sm("top"), 1)
                if L == 0 and s in (2, 3, 4) and ok(b - 3):
                    m = b - 3
                    tt = slice(2 * m, 2 * m + 2)
                    if s == 2:
                        dve.wait_ge(sm("top"), m + 1)
                        if m == 0:
                            dve.wait_ge(sm("consts"), 7)
                        dl(V.tensor_tensor(tmp[:, tt, :], lg[:, tt, :], v8[:, tt, 0:1].to_broadcast([P, 2, E8]), ALU.is_equal))
                        V.tensor_tensor(tmp[:, tt, :], tmp[:, tt, :], epri[:, :].unsqueeze(1).to_broadcast([P, 2, E8]), ALU.mult).then_inc(sm("pri"), 1)
                    elif s == 3:
                        dve.wait_ge(sm("pri"), m + 1)
                        V.reduce_max(m1[:, tt], tmp[:, tt, :], AX.X).then_inc(sm("first"), 1)
                    else:
                        dve.wait_ge(sm("first"), m + 1)
                        V.tensor_tensor(oh[:, tt, :], tmp[:, tt, :], m1[:, tt].unsqueeze(2).to_broadcast([P, 2, E8]), ALU.is_equal).then_inc(sm("oh_done"), 1)
                if L == 0 and s == 7 and ok(b - 3):
                    m = b - 3
                    tt = slice(2 * m, 2 * m + 2)
                    dve.wait_ge(sm("pos_done"), m + 1)
                    V.tensor_tensor(tmp[:, tt, :], misc[:, 0:2 * E8].rearrange("p (t e) -> p t e", t=2), oh[:, tt, :], ALU.mult).then_inc(sm("pos_evac"), 1)
                    if m == B - 1:
                        V.tensor_copy(cnt[:, :], misc[:, 2 * E8:3 * E8]).then_inc(sm("pos_evac"), 1)
                if L == 0 and s == 0 and ok(b - 4):
                    m = b - 4
                    tt = slice(2 * m, 2 * m + 2)
                    dve.wait_ge(sm("pos_evac"), m + 1)
                    V.reduce_sum(posf[:, tt], tmp[:, tt, :], AX.X).then_inc(sm("pos_red"), 1)
                if L == 1 and s == 0 and ok(b - 3):
                    m = b - 3
                    dve.wait_ge(*upto("xn2_ready", 1, m + 1))
                    V.reduce_max(am[:, 4, m:m + 1], flat(xn[:, 2 * m:2 * m + 2, :]), AX.X, apply_absolute_value=True).then_inc(sm("x_amax"), 1)
                if s == 2 and ok(b - 1):
                    dve.wait_ge(*upto("ott_done", L, b))
                    if b >= 2:
                        dve.wait_ge(*upto("ont_done", L, b - 1))
                    q4 = misc[:, :].rearrange("q (t a j c) -> q t a j c", t=2, a=2, j=4)
                    den_a = [q4[:, t, 0, :, 0:27].rearrange("q j (r c) -> q j r c", c=9) for t in range(2)]
                    for t in range(2):
                        V.reciprocal(rec[:, t, 0:12].rearrange("q (r j) -> q j r", j=4), den_a[t][:, :, :, DK])
                        last = V.reciprocal(rec[:, t, 12:16], q4[:, t, 1, :, DK])
                    dl(last)
                    for t in range(2):
                        V.tensor_tensor(on[:, t, 0:96].rearrange("q (r j d) -> q j r d", j=4, d=DK), den_a[t][:, :, :, 0:DK],
                                        rec[:, t, 0:12].rearrange("q (r j) -> q j r", j=4).unsqueeze(3).to_broadcast([P, 4, 3, DK]), ALU.mult)
                        last = V.tensor_tensor(on[:, t, 96:128].rearrange("q (j d) -> q j d", d=DK), q4[:, t, 1, :, 0:DK],
                                               rec[:, t, 12:16].unsqueeze(2).to_broadcast([P, 4, DK]), ALU.mult)
                    last.then_inc(sm("norm_done"), 1)
                if s == 4 and ok(b - 1):
                    dve.wait_ge(*upto("y_done", L, b))
                    xx = x[:, 2 * b - 2:2 * b, :]
                    V.tensor_tensor(xx, misc[:, 0:S].rearrange("p (t d) -> p t d", t=2), xx, ALU.add).then_inc(sm("x_done"), 1)

        def attention_pe(pe, L):
            free = []

            def take():
                for s_, v in free:
                    pe.wait_ge(s_, v)
                free.clear()

            for b, s in steps:
                if ok(b):
                    n = 8 * b + s
                    if s == 0:
                        pe.wait_ge(*upto("m_loaded", L, 32 * (b // 2 + 1), b % 2))
                    if n >= 2:
                        pe.wait_ge(*upto("exp_done", L, n - 1))
                    for r in range(2):
                        for t in range(TPB):
                            last = T.matmul(st_bank[n % 2][r][:, S * t:S * t + S], kstack[:, b % RING, r, s, P * t:P * t + P],
                                            qstack[:, b % RING, s, :], start=(t == 0), stop=(t == 1), skip_group_check=True)
                    last.then_inc(sm("st_done"), 1)
                n, p = scores_at(b, s)
                if ok(n):
                    if p == 0:
                        pe.wait_ge(*upto("q_loaded", L, 192 * (n // RING + 1), n % RING))
                        if L == 0 and n == 0:
                            pe.wait_ge(sm("k_first"), 192)
                        elif L == 0:
                            pe.wait_ge(sm(f"k_loaded{L}", n % RING), 32 * (n // RING + (n % RING > 0)))
                        else:
                            pe.wait_ge(sm(f"k_loaded{L}", n % RING), 32 * (n // RING + 1))
                    for r in range(2):
                        u = 16 * n + 2 * p + r
                        if u >= 2:
                            pe.wait_ge(*upto("red_done", L, u - 1))
                        for t in range(TPB):
                            last = T.matmul(a_bank[r][:, S * t:S * t + S], qstack[0:MROW, n % RING, p, P * t:P * t + P],
                                            kstack[0:MROW, n % RING, r, p, :], start=(t == 0), stop=(t == 1), skip_group_check=True)
                        last.then_inc(sm("a_done"), 1)
                if s == 1 and ok(b - 1) or s in (3, 5, 7) and ok(b):
                    n, q = (b - 1, 3) if s == 1 else (b, (s - 3) // 2)
                    pe.wait_ge(*upto("exp_done", L, 8 * n + 2 * q + 2))
                    if q == 0:
                        pe.wait_ge(*upto("v_ready", L, n + 1))
                        if n >= 1:
                            pe.wait_ge(*upto("ot_evac", L, n))
                    for t in range(TPB):
                        for j in range(4):
                            h = 4 * q + j
                            last = T.matmul(o_bank[32 * j:32 * j + 32, S * (q // 3):S * (q // 3) + S], vpad[:, n % 2, t, h, :],
                                            ex[:, (8 * n + 2 * q + j // 2) % 4, j % 2, t, :],
                                            start=(q in (0, 3) and t == 0), stop=(q in (2, 3) and t == 1), skip_group_check=True)
                    last.then_inc(sm("pv_done"), 1)
                if L == 0 and s == 0 and ok(b - 3):
                    n = b - 3
                    pe.wait_ge(*upto("xn2_ready", 0, n + 1))
                    take()
                    for t in range(TPB):
                        last = T.transpose(misc[:, P * t:P * t + P], xn[:, 2 * n + t, :], ident[:, :])
                    last.then_inc(sm("t2_done"), 1)
                    free.append((sm("t2_evac"), n + 1))
                if L == 0 and s == 1 and ok(b - 3):
                    n = b - 3
                    take()
                    for t in range(TPB):
                        last = T.matmul(misc[:, E8 * t:E8 * t + E8], t2[:, P * t:P * t + P], wr[:, :], start=(t == 0), stop=(t == 1), skip_group_check=True)
                    last.then_inc(sm("lg_done"), 1)
                    free.append((sm("lg_evac"), n + 1))
                if s == 2 and ok(b - 1):
                    pe.wait_ge(*upto("ot_evac", L, b))
                    take()
                    for t in range(TPB):
                        for a in range(2):
                            k = 2 * t + a
                            last = T.transpose(misc[:, P * k:P * k + P], ot[:, a, P * t:P * t + P], ident[:, :])
                    last.then_inc(sm("ott_done"), 1)
                    free.append(upto("norm_done", L, b))
                if s == 3 and ok(b - 1):
                    take()
                    for t in range(TPB):
                        last = T.transpose(misc[:, P * t:P * t + P], on[:, t, :], ident[:, :])
                    last.then_inc(sm("ont_done"), 1)
                    free.append(upto("ont_evac", L, b))
                if s == 4 and ok(b - 1):
                    take()
                    for t in range(TPB):
                        last = T.matmul(misc[:, P * t:P * t + P], ont[:, P * t:P * t + P], wo[L][:, :],
                                        start=(t == 0), stop=(t == 1), skip_group_check=True)
                    last.then_inc(sm("y_done"), 1)
                    free.append(upto("x_done", L, b))
                if s == 5 and ok(b + 1):
                    n = b + 1
                    pe.wait_ge(*upto("mx_ready", L, n + 1))
                    take()
                    for t in range(TPB):
                        last = T.matmul(misc[0:48, P * t:P * t + P], mparts[:, t, :, :, :].rearrange("q r c p -> q (r c p)"), identb[:, :],
                                        start=(t == 0), stop=(t == 1), skip_group_check=True)
                    last.then_inc(sm("mt_done"), 1)
                    free.append(upto("mt_evac", L, n + 1))
                if L == 0 and (b, s) == (B, 5):
                    keys1_pe(pe)
                if s == 6 and ok(b + 4):
                    n = b + 4
                    pe.wait_ge(*upto("xn_ready", L, n + 1))
                    take()
                    for t in range(TPB):
                        last = T.transpose(misc[:, P * t:P * t + P], xn[:, 2 * n + t, :], ident[:, :])
                    last.then_inc(sm("t_done"), 1)
                    free.append(upto("q_evac", L, 2 * n + 2) if L == 0 else (sm("xnt_evac"), n + 1))
                if L == 1 and s == 7 and ok(b + 4):
                    n = b + 4
                    take()
                    T.matmul(misc[:, 0:S], wq[:, :], xnt[:, :], start=True, stop=True).then_inc(sm("qp_done"), 1)
                    free.append(upto("q_evac", L, 2 * n + 2))
                if L == 0 and s == 7 and ok(b - 3):
                    n = b - 3
                    pe.wait_ge(sm("run_done"), n + 1)
                    if n == 0:
                        pe.wait_ge(sm("consts"), 7)
                    take()
                    for t in range(TPB):
                        T.matmul(misc[:, E8 * t:E8 * t + E8], before[:, :], oh[:, 2 * n + t, :], start=(t == 0), stop=False, skip_group_check=True)
                        last = T.matmul(misc[:, E8 * t:E8 * t + E8], ones[:, :], run[:, 2 * n + t, :], start=False, stop=(t == 1), skip_group_check=True)
                    if n == B - 1:
                        last = T.matmul(misc[:, 2 * E8:3 * E8], ones[:, :], run[:, NT, :], start=False, stop=True, skip_group_check=True)
                    last.then_inc(sm("pos_done"), 1)
                    free.append((sm("pos_evac"), n + 1 if n < B - 1 else B + 1))
            take()

        t_bank, h_bank, y_bank = ps[4], [ps[5], ps[6]], ps[7]

        def wbuf(i):
            return ex_flat[:, 2 * HID * (i % 2):2 * HID * (i % 2) + 2 * HID]

        def experts_sp(sp):
            sp.wait_ge(sm("consts"), 7)
            sp.wait_ge(sm("cnt_ready"), 1)
            sp.dma_start(xs_d[E8 * REG:E8 * REG + P, :], zt[:, :]).then_inc(sm("xs_zeroed"), 16)
            for e in range(E8):
                c = sp.value_load(cnt_i[0:1, e:e + 1], min_val=0, max_val=B * S)
                sp.dma_start(xs_d[bass.ds(c + e * REG, P), :], zt[:, :]).then_inc(sm("xs_zeroed"), 16)
            sp.wait_ge(sm("xs_zeroed"), 16 * (E8 + 1))
            sp.wait_ge(sm("scattered"), 16 * NT)
            sp.wait_ge(sm("tab_ready"), 1)
            for i in range(MT + 3):
                if i < MT:
                    r = sp.value_load(tbase[0:1, i:i + 1], min_val=0, max_val=E8 * REG)
                    if i >= 4:
                        sp.wait_ge(sm("st_done2"), i - 3)
                    sp.dma_start(xsb[:, i % 4, :], xs_d[bass.ds(r, P), :]).then_inc(sm("xs_loaded", i % 4), 16)
                if i == 3:
                    keys_sp(sp, 1)
                if i >= 3:
                    k = i - 3
                    sp.wait_ge(sm("ye_evac"), k + 1)
                    sp.dma_start(ys_d[k * P:k * P + P, :], ysb[:, k % 2, :]).then_inc(sm("y_stored", k % 2), 16)

        def experts_pool(pool):
            pool.wait_ge(sm("y_stored", 0), 16 * ((MT + 1) // 2))
            pool.wait_ge(sm("y_stored", 1), 16 * (MT // 2))
            pool.wait_ge(sm("tab_ready"), 1)

        def experts_act(act):
            act.wait_ge(sm("gdiff"), 1)
            C.activation(gate[:, :], gate[:, :], ACT.Exp).then_inc(sm("gexp"), 1)
            for i in range(MT + 1):
                if i < MT:
                    act.wait_ge(sm("st_done2"), i + 1)
                    if i >= 2:
                        act.wait_ge(sm("h_done"), i - 1)
                    C.copy(xst[:, i % 2, :], t_bank[:, 0:P]).then_inc(sm("st_evac2"), 1)
                if i >= 1:
                    k = i - 1
                    act.wait_ge(sm("h_done"), k + 1)
                    if k >= 2:
                        act.wait_ge(sm("ye_done"), k - 1)
                    C.activation(hg[:, k % 2, :], h_bank[k % 2][:, :], ACT.Gelu).then_inc(sm("g_done"), 1)
                if i == 16:
                    for k in range(3):
                        act.wait_ge(sm("wt_done"), k + 1)
                        C.copy(w3t[:, FF * k:FF * k + FF], ps[k][:, 0:FF]).then_inc(sm("wt_evac"), 1)

        def tables_dve(dve):
            def dl(ins):
                link(dve, ins, "dve_chain")
            dve.wait_ge(sm("pos_evac"), B + 1)
            V.tensor_copy(cnt_i[:, :], cnt[:, :]).then_inc(sm("cnt_ready"), 1)
            V.tensor_tensor(gate[:, :], v8[:, :, 1], v8[:, :, 0], ALU.subtract).then_inc(sm("gdiff"), 1)
            dl(V.tensor_scalar(ntile_i[:, :], cnt[:, :], 1.0 / P, 0.5 - 0.5 / P, ALU.mult, ALU.add))
            dl(V.tensor_copy(ntile[:, :], ntile_i[:, :]))
            dl(V.tensor_copy(incl[:, :], ntile[:, :]))
            for e in range(1, E8):
                dl(V.tensor_tensor(incl[:, e:e + 1], incl[:, e - 1:e], ntile[:, e:e + 1], ALU.add))
            dl(V.tensor_tensor(cmp_[:, :, :], incl[:, :].unsqueeze(1).to_broadcast([P, MT, E8]), tidx[:, :].unsqueeze(2).to_broadcast([P, MT, E8]), ALU.is_le))
            V.reduce_sum(texpf[:, :], cmp_[:, :, :], AX.X).then_inc(sm("texpf"), 1)
            dve.wait_ge(sm("texpf"), 1)
            dl(V.tensor_tensor(cmp_[:, :, :], cmp_[:, :, :], ntile[:, :].unsqueeze(1).to_broadcast([P, MT, E8]), ALU.mult))
            dl(V.reduce_sum(toff[:, :], cmp_[:, :, :], AX.X))
            dl(V.tensor_tensor(toff[:, :], tidx[:, :], toff[:, :], ALU.subtract))
            dl(V.tensor_scalar(toff[:, :], toff[:, :], float(P), None, ALU.mult))
            dl(V.scalar_tensor_tensor(toff[:, :], texpf[:, :], float(REG), toff[:, :], ALU.mult, ALU.add))
            dl(V.tensor_scalar(tbase[:, :], toff[:, :], float(E8 * REG), None, ALU.min))
            dl(V.tensor_scalar(texp[:, :], texpf[:, :], float(E8 - 1), None, ALU.min))
            dl(V.tensor_tensor(excl[:, :], incl[:, :], ntile[:, :], ALU.subtract))
            dl(V.tensor_scalar(excl[:, :], excl[:, :], float(P), None, ALU.mult))
            dve.wait_ge(sm("pos_red"), B)
            dl(V.tensor_tensor(tmp[:, :, :], oh[:, :, :], excl[:, :].unsqueeze(1).to_broadcast([P, NT, E8]), ALU.mult))
            dl(V.reduce_sum(rec[:, 0, :], tmp[:, :, :], AX.X))
            V.tensor_tensor(gslot[:, :], posf[:, :], rec[:, 0, :], ALU.add).then_inc(sm("tab_ready"), 1)

        def experts_dve(dve):
            def dl(ins):
                link(dve, ins, "dve_chain")
            tables_dve(dve)
            dve.wait_ge(sm("gexp"), 1)
            dl(V.tensor_scalar(gate[:, :], gate[:, :], 1.0, None, ALU.add))
            V.reciprocal(gate[:, :], gate[:, :]).then_inc(sm("gate_ready"), 1)
            dve.wait_ge(sm("ld_e"), 16 * 11)
            dve.wait_ge(*upto("pv_done", 0, 4 * B))
            for i in range(MT + 1):
                if i < MT:
                    if i >= 2:
                        dve.wait_ge(sm("ye_done"), i - 1)
                    e = dve.value_load(texp[0:1, i:i + 1], min_val=0, max_val=E8 - 1)
                    V.tensor_copy(wbuf(i), w12[:, bass.ds(e * (2 * HID), 2 * HID)]).then_inc(sm("w_copied"), 1)
                if 0 <= i < 4:
                    keys_dve(dve, 1, i)
                if 5 <= i < 9:
                    values1_dve(dve, i - 5)
                wb = w3[:, :].rearrange("p (n k) -> p n k", k=BLK)
                n3 = 3 * FF // BLK
                if i == 9:
                    dve.wait_ge(sm("ld_w"), 16 * 12)
                    dl(V.reduce_max(wam[:, :], wb, AX.X, apply_absolute_value=True))
                if i == 10:
                    dl(V.tensor_scalar(wam[:, :], wam[:, :], 1.0 / W_QMAX, TINY, ALU.mult, ALU.max))
                    dl(V.reciprocal(wrs[:, :], wam[:, :]))
                if i == 11:
                    dl(V.tensor_tensor(w3i[:, :].rearrange("p (n k) -> p n k", k=BLK), wb, wrs[:, :].unsqueeze(2).to_broadcast([P, n3, BLK]), ALU.mult))
                if i == 12:
                    V.tensor_tensor(wb, w3i[:, :].rearrange("p (n k) -> p n k", k=BLK), wam[:, :].unsqueeze(2).to_broadcast([P, n3, BLK]), ALU.mult).then_inc(sm("wq_done"), 1)
                if i >= 1:
                    k = i - 1
                    dve.wait_ge(sm("ye_done"), k + 1)
                    if k >= 2:
                        dve.wait_ge(sm("y_stored", k % 2), 16 * (k // 2))
                    V.tensor_copy(ysb[:, k % 2, :], y_bank[:, 0:P]).then_inc(sm("ye_evac"), 1)

        def experts_pe(pe):
            pe.wait_ge(*upto("red_done", 0, 16 * B))
            pe.wait_ge(*upto("ot_evac", 0, B))
            for i in range(MT + 1):
                if i < MT:
                    pe.wait_ge(sm("xs_loaded", i % 4), 16 * (i // 4 + 1))
                    if i >= 1:
                        pe.wait_ge(sm("st_evac2"), i)
                    T.transpose(t_bank[:, 0:P], xsb[:, i % 4, :], ident[:, :]).then_inc(sm("st_done2"), 1)
                if i >= 1:
                    k = i - 1
                    pe.wait_ge(sm("g_done"), k + 1)
                    if k >= 1:
                        pe.wait_ge(sm("ye_evac"), k)
                    for c in range(HC):
                        last = T.matmul(y_bank[:, 0:P], hg[:, k % 2, P * c:P * c + P], wbuf(k)[:, HID + P * c:HID + P * c + P],
                                        start=(c == 0), stop=(c == HC - 1))
                    last.then_inc(sm("ye_done"), 1)
                if i < MT:
                    pe.wait_ge(sm("st_evac2"), i + 1)
                    pe.wait_ge(sm("w_copied"), i + 1)
                    if i >= 2:
                        pe.wait_ge(sm("g_done"), i - 1)
                    for c in range(HC):
                        last = T.matmul(h_bank[i % 2][:, P * c:P * c + P], wbuf(i)[:, P * c:P * c + P], xst[:, i % 2, :],
                                        start=(c == 0), stop=(c == HC - 1), skip_group_check=True)
                    last.then_inc(sm("h_done"), 1)
                if 4 <= i < 8:
                    values1_pe(pe, i - 4)
                if i == 15:
                    pe.wait_ge(sm("wq_done"), 1)
                    pe.wait_ge(sm("d_v1"), 3)
                    for k in range(3):
                        for c in range(FC):
                            last = T.transpose(ps[k][:, P * c:P * c + P], w3[:, FF * k + P * c:FF * k + P * c + P], ident[:, :])
                        last.then_inc(sm("wt_done"), 1)

        xit = c28[:, 0:2048]
        gi = w12[:, 0:3072].bitcast(I16)
        ui = w12[:, 3072:6144].bitcast(I16)
        sig = [w12[:, 6144 + 512 * i:6656 + 512 * i] for i in range(4)]
        sq = [c28[:, 2048 + 256 * i:2304 + 256 * i].bitcast(U16) for i in range(4)]
        u_blocks = [kst_f[:, 512 * i:512 * i + 512] for i in range(NB, 16)] + [qst_f[:, 512 * i:512 * i + 512] for i in range(8)]

        def gb(i):
            return kst_f[:, 512 * i:512 * i + 512]

        def ub(i):
            return u_blocks[i]

        def gib(i):
            return gi[:, 512 * i:512 * i + 512]

        def uib(i):
            return ui[:, 512 * i:512 * i + 512]

        def col(i):
            return sc[:, i:i + 1]

        def ff_sp(sp):
            o_v = out.rearrange("b (t p) d -> p (b t) d", p=P)
            for c in range(4):
                sp.wait_ge(sm("out_ready"), c + 1)
                sp.dma_start(o_v[:, 4 * c:4 * c + 4, :], x[:, 4 * c:4 * c + 4, :]).then_inc(sm("stored"), 16)
            sp.wait_ge(sm("stored"), 64)

        def ff_pool(pool):
            def gmax(k):
                pool.wait_ge(sm("max_own"), k + 1)
                G.partition_all_reduce(col(k + 8), col(k), P, bass.bass_isa.ReduceOp.max).then_inc(sm("max_all"), 1)
            gmax(0)
            gmax(1)
            gmax(2)
            gmax(3)
            gmax(4)
            for i in range(NB):
                pool.wait_ge(sm("oq"), i + 1)
                G.tensor_scalar(gb(i), gb(i), -MAGIC, None, ALU.add).then_inc(sm("o_int"), 1)

        def ff_act(act):
            for c in range(4):
                act.wait_ge(sm("xt_done"), c + 1)
                C.activation(xit[:, 512 * c:512 * c + 512], ps[4 + c][:, :], ACT.Copy, bias=-MAGIC).then_inc(sm("xt_evac"), 1)

            def evac(i):
                act.wait_ge(sm("gu_done"), i + 1)
                C.copy(gb(i) if i < NB else ub(i - NB), ps[i % 4][:, :]).then_inc(sm("gu_evac"), 1)
            for i in range(NB + 2):
                evac(i)
            act.wait_ge(sm("scales"), 1)
            for i in range(NB):
                C.activation(gib(i), gb(i), ACT.Copy, scale=col(17)).then_inc(sm("gi_done"), 1)
                if NB + 2 + i < 2 * NB:
                    evac(NB + 2 + i)
                act.wait_ge(sm("gi_done"), i + 1)
                if i >= 4:
                    act.wait_ge(sm("sq_done"), i - 3)
                C.activation(sig[i % 4], gib(i), ACT.Sigmoid, scale=col(16)).then_inc(sm("sg_done"), 1)
            act.wait_ge(sm("scales"), 2)
            for i in range(NB):
                C.activation(uib(i), ub(i), ACT.Copy, scale=col(19)).then_inc(sm("ui_done"), 1)
            act.wait_ge(sm("scales"), 3)
            act.wait_ge(sm("p_done"), NB)
            for i in range(NB):
                C.activation(gib(i), gb(i), ACT.Copy, scale=col(21)).then_inc(sm("ai_done"), 1)
            act.wait_ge(sm("scales"), 4)
            for i in range(NB):
                C.activation(gb(i), ub(i), ACT.Identity, scale=col(23), bias=magic[:, :]).then_inc(sm("oq"), 1)

        def ff_dve(dve):
            def dl(ins):
                link(dve, ins, "dve_chain")

            def scale_of(m, true, dst, n):
                dl(V.tensor_tensor(col(m), col(m), col(true), ALU.mult))
                dl(V.tensor_scalar(col(dst), col(m), 1.0 / ACT_QMAX, TINY, ALU.mult, ALU.max))
                dl(V.reciprocal(col(dst + 1), col(dst)))
                V.tensor_tensor(col(dst + 1), col(dst + 1), col(true), ALU.mult).then_inc(sm("scales"), 1)
                dve.wait_ge(sm("scales"), n)

            dve.wait_ge(sm("x_amax"), B)
            V.reduce_max(col(0), am[:, 4, 0:B], AX.X).then_inc(sm("max_own"), 1)
            dve.wait_ge(sm("max_all"), 1)
            dl(V.tensor_scalar(col(14), col(8), 1.0 / ACT_QMAX, TINY, ALU.mult, ALU.max))
            dl(V.reciprocal(col(15), col(14)))
            for t in range(4):
                V.tensor_scalar(xn[:, 4 * t:4 * t + 4, :], xn[:, 4 * t:4 * t + 4, :], col(15), MAGIC, ALU.mult, ALU.add).then_inc(sm("xq_done"), 1)

            def amax(k, i, src):
                return V.reduce_max(am[:, k, i:i + 1], src, AX.X, apply_absolute_value=True)
            for i in range(NB):
                dve.wait_ge(sm("gu_evac"), i + 1)
                last = amax(0, i, gb(i))
            dl(last)
            V.reduce_max(col(1), am[:, 0, 0:NB], AX.X).then_inc(sm("max_own"), 1)
            for i in range(2):
                dve.wait_ge(sm("gu_evac"), NB + i + 1)
                amax(1, i, ub(i))
            dve.wait_ge(sm("max_all"), 2)
            scale_of(9, 14, 16, 1)
            for i in range(NB):
                if i + 2 < NB:
                    dve.wait_ge(sm("gu_evac"), NB + i + 3)
                    last = amax(1, i + 2, ub(i + 2))
                    if i + 2 == NB - 1:
                        dl(last)
                        V.reduce_max(col(2), am[:, 1, 0:NB], AX.X).then_inc(sm("max_own"), 1)
                dve.wait_ge(sm("sg_done"), i + 1)
                V.tensor_scalar(sq[i % 4], sig[i % 4], 65536.0, None, ALU.mult).then_inc(sm("sq_done"), 1)
                if i >= 1:
                    dve.wait_ge(sm("sq_done"), i)
                    V.tensor_tensor(gb(i - 1), gib(i - 1), sq[(i - 1) % 4], ALU.mult).then_inc(sm("p_done"), 1)
                if i >= 2:
                    dve.wait_ge(sm("p_done"), i - 1)
                    amax(2, i - 2, gb(i - 2))
            dve.wait_ge(sm("sq_done"), NB)
            V.tensor_tensor(gb(NB - 1), gib(NB - 1), sq[(NB - 1) % 4], ALU.mult).then_inc(sm("p_done"), 1)
            dve.wait_ge(sm("max_all"), 3)
            scale_of(10, 14, 18, 2)
            for i in range(NB - 2, NB):
                dve.wait_ge(sm("p_done"), i + 1)
                last = amax(2, i, gb(i))
            dl(last)
            dl(V.tensor_scalar(col(24), col(16), 1.0 / 65536.0, None, ALU.mult))
            V.reduce_max(col(3), am[:, 2, 0:NB], AX.X).then_inc(sm("max_own"), 1)
            dve.wait_ge(sm("max_all"), 4)
            scale_of(11, 24, 20, 3)
            for i in range(NB):
                dve.wait_ge(sm("ai_done"), i + 1)
                dve.wait_ge(sm("ui_done"), i + 1)
                V.tensor_tensor(ub(i), gib(i), uib(i), ALU.mult).then_inc(sm("au_done"), 1)
                if i >= 1:
                    dve.wait_ge(sm("au_done"), i)
                    amax(3, i - 1, ub(i - 1))
            dve.wait_ge(sm("au_done"), NB)
            dl(amax(3, NB - 1, ub(NB - 1)))
            dl(V.tensor_tensor(col(25), col(20), col(18), ALU.mult))
            V.reduce_max(col(4), am[:, 3, 0:NB], AX.X).then_inc(sm("max_own"), 1)
            dve.wait_ge(sm("max_all"), 5)
            scale_of(12, 25, 22, 4)
            for c in range(4):
                down_dve(dve, c)

        def down_dve(dve, c):
            dve.wait_ge(sm("d_done"), c + 1)
            V.scalar_tensor_tensor(x[:, 4 * c:4 * c + 4, :], ps[4 + c][:, :].rearrange("p (t d) -> p t d", t=4), col(22),
                                   x[:, 4 * c:4 * c + 4, :], ALU.mult, ALU.add).then_inc(sm("out_ready"), 1)

        def ff_pe(pe):
            pe.wait_ge(*upto("exp_done", 1, 8 * B))
            pe.wait_ge(*upto("red_done", 1, 16 * B))
            pe.wait_ge(*upto("ot_evac", 1, B))
            for c in range(4):
                pe.wait_ge(sm("xq_done"), c + 1)
                for t in range(4):
                    last = T.transpose(ps[4 + c][:, P * t:P * t + P], xn[:, 4 * c + t, :], ident[:, :])
                last.then_inc(sm("xt_done"), 1)
            pe.wait_ge(sm("wt_evac"), 3)
            for i in range(2 * NB):
                k, j = i // NB, i % NB
                n, c = j // FC, j % FC
                pe.wait_ge(sm("xt_evac"), n + 1 if i < NB else 4)
                if i >= 4:
                    pe.wait_ge(sm("gu_evac"), i - 3)
                T.matmul(ps[i % 4][:, :], w3t[:, FF * k + P * c:FF * k + P * c + P], xit[:, 512 * n:512 * n + 512], start=True, stop=True).then_inc(sm("gu_done"), 1)
            for c in range(4):
                pe.wait_ge(sm("o_int"), FC * c + FC)
                for t in range(4):
                    for f in range(FC):
                        k = P * t
                        last = T.matmul(ps[4 + c][:, P * t:P * t + P], gb(FC * c + f)[:, k:k + P], w3t[:, 2 * FF + P * f:2 * FF + P * f + P],
                                        start=(f == 0 and t == 0), stop=(f == FC - 1 and t == 3), skip_group_check=True)
                last.then_inc(sm("d_done"), 1)

        with nc.Block() as block:
            @block.sync
            def _(sp):
                prologue_sp(sp)
                attention_sp(sp, 0)
                experts_sp(sp)
                attention_sp(sp, 1)
                ff_sp(sp)

            @block.gpsimd
            def _(pool):
                prologue_pool(pool)
                attention_pool(pool, 0)
                experts_pool(pool)
                attention_pool(pool, 1)
                ff_pool(pool)

            @block.scalar
            def _(act):
                prologue_act(act)
                attention_act(act, 0)
                experts_act(act)
                attention_act(act, 1)
                ff_act(act)

            @block.vector
            def _(dve):
                prologue_dve(dve)
                attention_dve(dve, 0)
                experts_dve(dve)
                attention_dve(dve, 1)
                ff_dve(dve)

            @block.tensor
            def _(pe):
                keys0_pe(pe)
                attention_pe(pe, 0)
                experts_pe(pe)
                attention_pe(pe, 1)
                ff_pe(pe)


_INS = ["x", "ctx_1024", "L0_xattn_w_out", "L0_xattn_b_out", "L0_ffn_Wr", "L0_ffn_W1", "L0_ffn_W2", "L1_xattn_W_Q", "L1_xattn_b_Q",
        "L1_xattn_W_K", "L1_xattn_b_K", "L1_xattn_W_V", "L1_xattn_b_V", "L1_xattn_W_O", "L1_xattn_b_O", "L1_ffn_w_gate",
        "L1_ffn_w_up", "L1_ffn_w_down"]


def kernel(**inputs):
    import numpy as _np
    import concourse.bacc as _bacc
    from concourse import mybir as _mybir
    from concourse.bass_utils import run_bass_kernel_spmd as _run

    nc = _bacc.Bacc("TRN2", target_bir_lowering=False, num_devices=1)
    arrays, aps = {}, {}
    laid = {n: _np.ascontiguousarray(inputs[n]) for n in _INS}
    laid["w_out_t"] = _np.ascontiguousarray(_np.asarray(laid.pop("L0_xattn_w_out")).T)
    order = _np.arange(D).reshape(PAIRS, 2, DK).transpose(1, 2, 0).reshape(-1)
    laid["w_q"] = _np.ascontiguousarray(laid.pop("L1_xattn_W_Q")[:, order])
    laid["w_k"] = _np.ascontiguousarray(laid.pop("L1_xattn_W_K")[:, order])
    laid["b_q"] = _np.ascontiguousarray(laid.pop("L1_xattn_b_Q")[order])
    laid["b_k"] = _np.ascontiguousarray(laid.pop("L1_xattn_b_K")[order])
    for name, a in laid.items():
        arrays[f"in_{name}"] = a
        aps[name] = nc.dram_tensor(f"in_{name}", a.shape, _mybir.dt.from_np(a.dtype), kind="ExternalInput").ap()
    out = nc.dram_tensor("out_0", (B, S, D), F32, kind="ExternalOutput").ap()
    emit(nc, aps, out)
    r = _run(nc, [arrays], core_ids=[0])
    return r.results[0]["out_0"]
```

```python
from contextlib import ExitStack

import concourse.bass as bass
from concourse import mybir

ALU = mybir.AluOpType
ACT = mybir.ActivationFunctionType
AX = mybir.AxisListType
F32 = mybir.dt.float32
BF16 = mybir.dt.bfloat16
I32 = mybir.dt.int32
I16 = mybir.dt.int16
U16 = mybir.dt.uint16

P = 128
B, S, D = 8, 256, 128
H, DK = 16, 8
NT = B * S // P
TPB = S // P
PAIRS = H // 2
QUADS = H // 4
E8 = 8
HID = 512
HC = HID // P
REG = B * S + P
MT = NT + E8 - 1
FF = 384
FC = FF // P
BLK = 32
EPS = 1e-5
ACT_QMAX = 2.0 ** 15 - 1.0
W_QMAX = 2.0 ** 3 - 1.0
TINY = 1e-12
Q_SLOT = (0, 0, 0, 1, 1, 2)
K_SLOT = (0, 1, 2, 0, 1, 0)
SLOTS = len(Q_SLOT)
SROW = 2 * DK
SROWS = SLOTS * SROW
MROW = P - 2 * 3
RING = 4
ISQ = float(DK) ** -0.5
MAGIC = 1.5 * 2.0 ** 23
NB = FC * B * S // 512


def emit(nc, A, out):
    ctx = ExitStack()
    with ctx:
        def sb(name, shape, dt=F32):
            return ctx.enter_context(nc.sbuf_tensor(name, shape, dt))

        sems = {}

        def sm(name, i=""):
            key = f"{name}_{i}"
            if key not in sems:
                sems[key] = ctx.enter_context(nc.semaphore(key))
            return sems[key]

        LN_LEN = 15
        PER_LAYER = dict(
            ln_step=LN_LEN * (B + 6), st_done=16 * B, exp_done=16 * B, a_done=16 * B, red_done=16 * B, pv_done=4 * B,
            parts_ready=B, q_evac=2 * B, q_loaded=16 * SLOTS * (B // RING), mt_evac=B, mt_done=B, mx_ready=B,
            m_loaded=16 * (B // 2), v_ready=B, xn_ready=B, bias_added=B, xn2_ready=B, t_done=B, ot_evac=B,
            ont_done=B, ont_evac=B, ott_done=B, norm_done=B, y_done=B, x_done=B)

        def upto(name, L, n, i=""):
            return sm(name, i), n + L * PER_LAYER[name]

        T, V, G, C = nc.tensor, nc.vector, nc.gpsimd, nc.scalar

        ident = sb("ident", [P, P])
        identb = sb("identb", [P, P], BF16)
        ones = sb("ones", [P, P], BF16)
        before = sb("before", [P, P], BF16)
        x = sb("x", [P, NT, D])
        xn = sb("xn", [P, NT, D])
        ctxt = sb("ctxt", [P, NT, D])
        v1 = sb("v1", [P, NT, D])
        kstack = sb("kstack", [P, RING, 2, PAIRS, S], BF16)
        qstack = sb("qstack", [P, RING, PAIRS, S], BF16)
        qparts = sb("qparts", [P, 2, 3, S], BF16)
        qf = sb("qf", [P, 2, S])
        qr = sb("qr", [P, S])
        xnt = sb("xnt", [P, S])
        ex = sb("ex", [P, 4, 2, TPB, S])
        vpad = sb("vpad", [P, 2, TPB, H, 32])
        mx = sb("mx", [P, 2, TPB, 2, PAIRS])
        mr = sb("mr", [P, TPB, 2, PAIRS])
        mparts = sb("mparts", [P, TPB, 2, 3, PAIRS], BF16)
        mt = sb("mt", [2 * 3 * PAIRS, 2, S], BF16)
        ot = sb("ot", [P, 2, S])
        rec = sb("rec", [P, TPB * 8, 3])
        on = sb("on", [P, TPB, D])
        ont = sb("ont", [P, S])
        xsb = ot[:, :, :].rearrange("p a (b d) -> p (a b) d", b=2)
        xst = ont[:, :].rearrange("p (a t) -> p a t", a=2)
        ysb = on
        wo = [sb("wo0", [P, D]), sb("wo1", [P, D])]
        bo = [sb("bo0", [P, D]), sb("bo1", [P, D])]
        wq = sb("wq", [P, D])
        wk = sb("wk", [P, D])
        wv = sb("wv", [P, D])
        bv = sb("bv", [P, D])
        bqk = sb("bqk", [P, 2])
        stat = sb("stat", [P, 2, 4, 6])
        mv = sb("mv", [P, 2, 4, 2])
        nw = sb("nw", [P, 2, 4, 4])
        nmr = sb("nmr", [P, 2, 4])
        w12 = sb("w12", [P, E8 * 2 * HID])
        c28 = sb("c28", [P, 7168])
        ctx_t = c28[:, 0:2048]
        kr = c28[:, 2048:4096]
        kp = c28[:, 4096:7168].bitcast(BF16).rearrange("p (c t) -> p c t", c=3)
        t2 = sb("t2", [P, S])
        wr = sb("wr", [P, E8])
        epri = sb("epri", [P, E8])
        tidx = sb("tidx", [P, MT])
        lg = sb("lg", [P, NT, E8])
        v8 = sb("v8", [P, NT, E8])
        oh = sb("oh", [P, NT, E8], BF16)
        run = sb("run", [P, NT + 1, E8], BF16)
        tmp = sb("tmp", [P, NT, E8])
        m1 = sb("m1", [P, NT])
        posf = sb("posf", [P, NT])
        ebase = sb("ebase", [P, NT])
        gate = sb("gate", [P, NT])
        ntile = sb("ntile", [P, E8])
        ntile_i = sb("ntile_i", [P, E8], I16)
        cnt = sb("cnt", [P, E8])
        cnt_i = sb("cnt_i", [P, E8], I32)
        incl = sb("incl", [P, E8])
        excl = sb("excl", [P, E8])
        slot = sb("slot", [P, NT], I32)
        gslot = sb("gslot", [P, NT], I32)
        cmp_ = sb("cmp_", [P, MT, E8])
        texpf = sb("texpf", [P, MT])
        toff = sb("toff", [P, MT])
        texp = sb("texp", [P, MT], I32)
        tbase = sb("tbase", [P, MT], I32)
        zt = sb("zt", [P, D])
        hg = sb("hg", [P, 2, HID])
        w3 = sb("w3", [P, 3 * FF])
        w3t = sb("w3t", [P, 3 * FF])
        w3i = sb("w3i", [P, 3 * FF], I16)
        wam = sb("wam", [P, 3 * FF // BLK])
        wrs = sb("wrs", [P, 3 * FF // BLK])
        sc = sb("sc", [P, 26])
        spare = sb("spare", [P, 1])
        am = sb("am", [P, 5, NB])
        ex_flat = ex[:, :, :, :, :].rearrange("p a b c d -> p (a b c d)")
        neg = ex_flat[0:3 * RING, 0:PAIRS * S // 2].bitcast(BF16)
        kst_f = kstack[:, :, :, :, :].rearrange("p a b c d -> p (a b c d)").bitcast(F32)
        qst_f = qstack[:, :, :, :].rearrange("p a b c -> p (a b c)").bitcast(F32)

        kd = [nc.dram_tensor(f"kd{i}", (SROWS, PAIRS, B * S), BF16, kind="Internal").ap() for i in range(2)]
        xs_d = nc.dram_tensor("xs_d", (E8 * REG + P, D), F32, kind="Internal").ap()
        ys_d = nc.dram_tensor("ys_d", (MT * P, D), F32, kind="Internal").ap()

        ps = [ctx.enter_context(nc.psum_tensor(f"ps{i}", [P, 512], F32)) for i in range(8)]
        st_bank, a_bank = ps[0:3], [ps[4], ps[5], ps[3]]
        o_bank, misc = ps[6], ps[7]

        x_v = A["x"].rearrange("b (t p) d -> p (b t) d", p=P)
        c_v = A["ctx_1024"].rearrange("b (t p) d -> p (b t) d", p=P)

        chains = {}

        def link(eng, ins, name):
            chains[name] = chains.get(name, 0) + 1
            ins.then_inc(sm(name), 1)
            eng.wait_ge(sm(name), chains[name])

        def perm(ap):
            return ap.rearrange("a (p r d) -> a d r p", r=2, d=DK)

        def as_perm(ap):
            return ap.rearrange("a (d r p) -> a d r p", r=2, d=DK)

        def flat(ap):
            return ap.rearrange("p a b -> p (a b)")

        def keys0_pe(pe):
            pe.wait_ge(sm("ident"), 1)
            keys0_chunks_pe(pe, (0, 1))

        def keys0_chunks_pe(pe, chunks):
            for c in chunks:
                pe.wait_ge(sm("cperm"), 4 * c + 4)
                for t in range(4):
                    last = T.transpose(ps[c][:, P * t:P * t + P], xn[:, 4 * c + t, :], ident[:, :])
                last.then_inc(sm("p_k", 0), 1)

        def keys1_pe(pe):
            pe.wait_ge(*upto("exp_done", 0, 16 * B))
            for c in range(4):
                for t in range(4):
                    last = T.transpose(ps[c][:, P * t:P * t + P], ctxt[:, 4 * c + t, :], ident[:, :])
                last.then_inc(sm("p_ct"), 1)
            pe.wait_ge(sm("ld_w"), 16 * 12)
            for c in range(4):
                pe.wait_ge(sm("a_ct"), c + 1)
                T.matmul(ps[c][:, :], wk[:, :], ctx_t[:, 512 * c:512 * c + 512], start=True, stop=True).then_inc(sm("p_k", 1), 1)

        def keys1_act(act):
            for c in range(4):
                act.wait_ge(sm("p_ct"), c + 1)
                C.copy(ctx_t[:, 512 * c:512 * c + 512], ps[c][:, :]).then_inc(sm("a_ct"), 1)
            act.wait_ge(sm("ld_w"), 16 * 12)
            act.wait_ge(sm("kd_stored", 0), 16 * SLOTS)
            for c in range(4):
                act.wait_ge(sm("p_k", 1), c + 1)
                for dst in (kr[:, 512 * c:512 * c + 512], kp[:, 0, 512 * c:512 * c + 512]):
                    C.activation(dst, ps[c][:, :], ACT.Identity, bias=bqk[:, 1:2]).then_inc(sm("a_k", 1), 1)

        def keys0_dve(dve, c):
            L, col = 0, slice(512 * c, 512 * c + 512)
            dve.wait_ge(sm("a_k", L), c + 1)
            link(dve, V.tensor_tensor(kr[:, col], ps[c][:, :], kp[:, 0, col], ALU.subtract), "dve_chain")
            link(dve, V.tensor_copy(kp[:, 1, col], kr[:, col]), "dve_chain")
            V.tensor_tensor(kp[:, 2, col], kr[:, col], kp[:, 1, col], ALU.subtract).then_inc(sm("d_k", L), 1)

        def keys_sp(sp, L):
            for i in range(SLOTS):
                keys_slot_sp(sp, L, i, slice(2 * S if L == 0 else 0, B * S), "kd_stored")

        def keys_slot_sp(sp, L, i, tokens, done):
            chunks = tokens.stop // 512 if tokens.stop > 512 else 1
            sp.wait_ge(sm("a_k", L), chunks * (1 + L))
            sp.wait_ge(sm("d_k", L), chunks)
            sp.dma_start(kd[L][SROW * i:SROW * i + SROW, :, tokens].rearrange("q p t -> (q p) t"), kp[:, K_SLOT[i], tokens]).then_inc(sm(done, L), 16)

        def values1_pe(pe, c):
            pe.wait_ge(sm("a_k", 1), 2 * c + 2)
            for t in range(4):
                k = P * (4 * c + t)
                last = T.matmul(ps[c][:, P * t:P * t + P], ctx_t[:, k:k + P], wv[:, :], start=(t == 0), stop=(t == 3), skip_group_check=True)
            last.then_inc(sm("p_v1"), 1)

        def values1_dve(dve, c):
            dve.wait_ge(sm("p_v1"), c + 1)
            V.tensor_tensor(v1[:, 4 * c:4 * c + 4, :], ps[c][:, :].rearrange("p (t d) -> p t d", t=4),
                            bv[:, :].unsqueeze(1).to_broadcast([P, 4, D]), ALU.add).then_inc(sm("d_v1"), 1)

        def prologue_sp(sp):
            for i in range(4):
                sp.dma_start(ctxt[:, 4 * i:4 * i + 4, :], c_v[:, 4 * i:4 * i + 4, :]).then_inc(sm("ld_ctx", i), 16)
            sp.wait_ge(sm("neg"), 1)
            sp.wait_ge(sm("kzero"), 4)
            for r in range(2):
                k = MROW + 3 * r
                sp.dma_start(kstack[k:k + 3, :, r, :, :].rearrange("k a p t -> k a (p t)"), neg).then_inc(sm("neg_stored"), 16)
            sp.wait_ge(sm("qzero"), 2)
            for n in range(2):
                for i in range(SLOTS):
                    keys_slot_sp(sp, 0, i, slice(S * n, S * n + S), ("kd_first", "kd_second")[n])

        def first_keys_sp(sp):
            sp.wait_ge(sm("kd_first", 0), 16 * SLOTS)
            for r in range(2):
                sp.dma_start(kstack[r:SROWS:2, 0, r, :, :], kd[0][r:SROWS:2, :, 0:S]).then_inc(sm("k_first"), 16)

        def prologue_act(act):
            act.dma_start(x[:, 0:4, :], x_v[:, 0:4, :]).then_inc(sm("ld_x", 0), 16)
            act.dma_start(x[:, 4:16, :], x_v[:, 4:16, :]).then_inc(sm("ld_x", 1), 16)
            with nc.allow_non_contiguous_dma(reason="two vectors of 128 elements"):
                for i, n in enumerate(("b_q", "b_k")):
                    act.dma_start(bqk[:, i:i + 1], A[n].unsqueeze(1)).then_inc(sm("ld_w"), 16)
            for dst, n in ((wq, "w_q"), (wk, "w_k"), (wv, "L1_xattn_W_V"), (wo[0], "w_out_t"), (wo[1], "L1_xattn_W_O"), (wr, "L0_ffn_Wr")):
                act.dma_start(dst[:, :], A[n]).then_inc(sm("ld_w"), 16)
            for dst, n in ((bo[0], "L0_xattn_b_out"), (bo[1], "L1_xattn_b_O"), (bv, "L1_xattn_b_V")):
                act.dma_start(dst[:, :], A[n].partition_broadcast(P)).then_inc(sm("ld_w"), 16)
            act.dma_start(w3[:, 2 * FF:3 * FF], A["L1_ffn_w_down"]).then_inc(sm("ld_w"), 16)
            keys0_chunks_act(act, (0, 1))

        def keys0_chunks_act(act, chunks):
            for c in chunks:
                act.wait_ge(sm("p_k", 0), c + 1)
                C.copy(kp[:, 0, 512 * c:512 * c + 512], ps[c][:, :]).then_inc(sm("a_k", 0), 1)

        def prologue_pool(pool):
            G.memset(ident[:, :], 0.0).then_inc(sm("pool_chain"), 1)
            chains["pool_chain"] = 1
            pool.wait_ge(sm("pool_chain"), 1)
            G.affine_select(out=ident[:, :], in_=ident[:, :], compare_op=ALU.not_equal, fill=1.0, base=0,
                            pattern=[[-1, P]], channel_multiplier=1).then_inc(sm("ident"), 1)
            for i in (2, 3):
                G.memset(kst_f[:, 2048 * i:2048 * i + 2048], 0.0).then_inc(sm("kzero"), 1)
            for i in range(2):
                G.memset(qst_f[:, 2048 * i:2048 * i + 2048], 0.0).then_inc(sm("qzero"), 1)
            G.memset(ones[:, :], 1.0).then_inc(sm("consts"), 1)
            G.memset(zt[:, :], 0.0).then_inc(sm("consts"), 1)
            G.memset(run[:, 0, :], 0.0).then_inc(sm("consts"), 1)
            G.iota(epri[:, :], [[-1, E8]], base=E8, channel_multiplier=0, allow_small_or_imprecise_dtypes=True).then_inc(sm("consts"), 1)
            G.iota(tidx[:, :], [[1, MT]], base=0, channel_multiplier=0, allow_small_or_imprecise_dtypes=True).then_inc(sm("consts"), 1)
            pool.wait_ge(sm("ident"), 1)
            G.tensor_copy(identb[:, :], ident[:, :]).then_inc(sm("consts"), 1)
            pool.wait_ge(sm("consts"), 6)
            G.affine_select(out=before[:, :], in_=ones[:, :], compare_op=ALU.is_gt, fill=0.0, base=0, pattern=[[1, P]],
                            channel_multiplier=-1).then_inc(sm("consts"), 1)

        def prologue_pool_late(pool):
            link(pool, G.memset(vpad[:, :, :, :, :], 0.0), "pool_chain")
            for q in range(QUADS):
                for o in ((9 * q + DK,) if q < 3 else (DK, 9 + DK, 18 + DK)):
                    last = G.memset(vpad[:, :, :, 4 * q:4 * q + 4, o:o + 1], 1.0)
            link(pool, last, "pool_chain")

        def prologue_dve(dve):
            V.memset(neg, -1.0).then_inc(sm("neg"), 1)
            for i in (0, 1):
                V.memset(kst_f[:, 2048 * i:2048 * i + 2048], 0.0).then_inc(sm("kzero"), 1)
            cperm_dve(dve, range(8))

        def cperm_dve(dve, tiles):
            for t in tiles:
                if t % 4 == 0:
                    dve.wait_ge(sm("ld_ctx", t // 4), 16)
                V.tensor_copy(as_perm(xn[:, t, :]), perm(ctxt[:, t, :])).then_inc(sm("cperm"), 1)

        first_b, last_b = -5, B + 5
        steps = [(b, s) for b in range(first_b, last_b) for s in range(8)]
        LNB = -4

        def ok(b):
            return 0 <= b < B

        def gathered_at(b, s):
            if b < 0:
                return ((0, 1) if b == first_b else (b + 6,)) if s == 6 else ()
            return (b + 5,) if s == 1 and ok(b + 5) and b >= 1 else ()

        def transposed_at(b, s):
            return b + 3 if s == (3 if b < 0 else 6) and ok(b + 3) else None

        def queries_at(b, s):
            return b + 3 if s == (3 if b < 0 else 7) and ok(b + 3) else None

        def parts_at(b, s):
            n = b + 3 if b < 0 else b + 2
            return n if s == (1 if b < -1 else 4 if b < 0 else 0) and ok(n) and (b < 0 or n >= 3) else None

        def scores_at(b, s):
            g = 8 * b + s + 12
            return g // 8, g % 8

        def ln_cols(b):
            return (0 if ok(b + 4) else 2), (4 if ok(b - 2) else 2)

        def attention_sp(sp, L):
            for b, s in steps:
                if L == 0 and (b, s) == (-3, 0):
                    first_keys_sp(sp)
                n = b + 3 if b < 0 else b + 2
                if s == 0 and ok(n) and (b < 0 or n >= 3) and (L == 1 or b >= -2):
                    if n >= RING:
                        sp.wait_ge(*upto("st_done", L, 16 * (n - RING) + 16))
                    if L == 1 and n == 0:
                        sp.wait_ge(*upto("st_done", 0, 16 * B))
                    if L == 1 or n > 0:
                        sp.wait_ge(sm("kd_second" if L == 0 and n == 1 else "kd_stored", L), 16 * SLOTS)
                        for r in range(2):
                            sp.dma_start(kstack[r:SROWS:2, n % RING, r, :, :], kd[L][r:SROWS:2, :, S * n:S * n + S]).then_inc(sm(f"k_loaded{L}", n % RING), 16)
                n = parts_at(b, s) if b != -1 else 2 if s == 7 else None
                if n is not None:
                    sp.wait_ge(*upto("q_evac", L, 2 * n + 2))
                    for i, c in enumerate(Q_SLOT):
                        if i == 3:
                            sp.wait_ge(*upto("parts_ready", L, n + 1))
                        k = SROW * i
                        sp.dma_start(qstack[k:k + SROW, n % RING, :, :], qparts[:, n % 2, c, :]).then_inc(sm("q_loaded", n % RING), 16)
                if L == 0 and (b, s) == (-2, 2):
                    keys_sp(sp, 0)
                if L == 0 and s == 2 and ok(b):
                    sp.dma_start(w12[:, 2 * HID * b:2 * HID * b + HID], A["L0_ffn_W1"][b]).then_inc(sm("ld_e"), 16)
                    o = 2 * HID * b + HID
                    sp.dma_start(w12[:, o:o + HID].rearrange("p (c d) -> p c d", c=HC), A["L0_ffn_W2"][b].rearrange("(c p) d -> p c d", p=P)).then_inc(sm("ld_e"), 16)
                if L == 0 and (b, s) == (0, 3):
                    for i, n in enumerate(("L1_ffn_w_gate", "L1_ffn_w_up")):
                        sp.dma_start(w3[:, FF * i:FF * i + FF].rearrange("p (c h) -> p c h", c=FC), A[n].rearrange("(c p) h -> p c h", p=P)).then_inc(sm("ld_e"), 16)
                if s == 6 and ok(b + 1):
                    n = b + 1
                    sp.wait_ge(*upto("mt_evac", L, n + 1))
                    sp.dma_start(qstack[MROW:P, n % RING, :, :], mt[:, n % 2, :]).then_inc(sm("m_loaded", n % 2), 16)

        def attention_pool(pool, L):
            vsrc = ctxt if L == 0 else v1

            def pl(ins):
                link(pool, ins, "pool_chain")
            for b, s in steps:
                if s == 2 and ok(b + 3):
                    n = b + 3
                    k = (b - 1) % 2
                    if L == 0:
                        pool.wait_ge(sm("p_k", 0), (2 * n + 1) // 4 + 1)
                    pool.wait_ge(*upto("ln_step", L, LN_LEN * (b - LNB)))
                    for i in range(2):
                        t = 2 * n + i
                        dst = xn[:, t, :]
                        last = G.tensor_scalar(as_perm(dst) if L == 0 else dst, perm(x[:, t, :]) if L == 0 else x[:, t, :],
                                               nw[:, k, 1, i:i + 1], nmr[:, k, i:i + 1], ALU.mult, ALU.add)
                    last.then_inc(sm("xn_ready"), 1)
                    pool.wait_ge(*upto("xn_ready", L, n + 1))
                    if L == 0 and n == 0:
                        pool.wait_ge(sm("ld_w"), 16 * 12)
                    G.tensor_tensor(x[:, 2 * n:2 * n + 2, :], x[:, 2 * n:2 * n + 2, :],
                                    bo[L][:, :].unsqueeze(1).to_broadcast([P, 2, D]), ALU.add).then_inc(sm("bias_added"), 1)
                if L == 0 and (b, s) == (-2, 6):
                    prologue_pool_late(pool)
                if s == 3 and ok(b + 1):
                    n = b + 1
                    if n >= 2:
                        pool.wait_ge(*upto("pv_done", L, 4 * (n - 2) + 4))
                    elif L == 0:
                        pool.wait_ge(sm("ld_ctx", 0), 16)
                    else:
                        pool.wait_ge(*upto("pv_done", 0, 4 * B))
                        pool.wait_ge(sm("d_v1"), 4)
                    if L == 0 and n % 2 == 0:
                        pool.wait_ge(sm("ld_ctx", n // 2), 16)
                    for q in range(QUADS):
                        o = 9 * (q % 3)
                        last = G.tensor_copy(vpad[:, n % 2, :, 4 * q:4 * q + 4, o:o + DK],
                                             vsrc[:, 2 * n:2 * n + 2, 32 * q:32 * q + 32].rearrange("p t (j d) -> p t j d", j=4))
                    last.then_inc(sm("v_ready"), 1)
                if s == 4 and ok(b + 1):
                    n = b + 1
                    pool.wait_ge(*upto("red_done", L, 16 * n + 16))
                    if n >= 1:
                        pool.wait_ge(*upto("mt_done", L, n))
                    m_, r_ = mx[:, n % 2], mr[:, :, :, :]
                    pl(G.tensor_scalar(mparts[:, :, :, 0, :], m_, 1.0, None, ALU.mult))
                    pl(G.tensor_tensor(r_, m_, mparts[:, :, :, 0, :], ALU.subtract))
                    pl(G.tensor_scalar(mparts[:, :, :, 1, :], r_, 1.0, None, ALU.mult))
                    G.tensor_tensor(mparts[:, :, :, 2, :], r_, mparts[:, :, :, 1, :], ALU.subtract).then_inc(sm("mx_ready"), 1)
                n = parts_at(b, s)
                if n is not None and b >= 0:
                    if n == 3:
                        pool.wait_ge(*upto("parts_ready", L, n))
                    pool.wait_ge(*upto("q_evac", L, 2 * n + 2))
                    if n >= 2:
                        pool.wait_ge(*upto("q_loaded", L, 16 * SLOTS * ((n - 2) // RING + 1), (n - 2) % RING))
                    pl(G.tensor_tensor(qr[:, :], qf[:, n % 2, :], qparts[:, n % 2, 0, :], ALU.subtract))
                    pl(G.tensor_scalar(qparts[:, n % 2, 1, :], qr[:, :], 1.0, None, ALU.mult))
                    G.tensor_tensor(qparts[:, n % 2, 2, :], qr[:, :], qparts[:, n % 2, 1, :], ALU.subtract).then_inc(sm("parts_ready"), 1)
                if L == 0 and s == 5 and ok(b - 3):
                    n = b - 3
                    pool.wait_ge(sm("oh_done"), n + 1)
                    pl(G.tensor_tensor(run[:, 2 * n + 1, :], run[:, 2 * n, :], oh[:, 2 * n, :], ALU.add))
                    G.tensor_tensor(run[:, 2 * n + 2, :], run[:, 2 * n + 1, :], oh[:, 2 * n + 1, :], ALU.add).then_inc(sm("run_done"), 1)
                    pool.wait_ge(sm("run_done"), n + 1)
                if L == 1:
                    for m in gathered_at(b, s):
                        for t in (2 * m, 2 * m + 1):
                            G.indirect_dma_start(out=ctxt[:, t, :], out_offset=None, in_=ys_d,
                                                 in_offset=bass.IndirectOffsetOnAxis(ap=gslot[:, t:t + 1], axis=0)).then_inc(sm("gathered", m), 16)
                if s == 7 and ok(b - 2):
                    n = b - 2
                    pool.wait_ge(*upto("ln_step", L, LN_LEN * (b - LNB + 1)))
                    for i in range(2):
                        t = 2 * n + i
                        last = G.tensor_scalar(xn[:, t, :], x[:, t, :], nw[:, b % 2, 1, 2 + i:3 + i], nmr[:, b % 2, 2 + i:3 + i], ALU.mult, ALU.add)
                    last.then_inc(sm("xn2_ready"), 1)
                    pool.wait_ge(*upto("xn2_ready", L, n + 1))
                if L == 0 and s == (1 if b < B else 7) and ok(b - 4):
                    n = b - 4
                    t = slice(2 * n, 2 * n + 2)
                    pool.wait_ge(sm("pos_red"), n + 1)
                    pl(G.tensor_scalar(ebase[:, t], m1[:, t], -float(REG), float(E8 * REG), ALU.mult, ALU.add))
                    pl(G.tensor_tensor(ebase[:, t], posf[:, t], ebase[:, t], ALU.add))
                    pl(G.tensor_copy(slot[:, t], ebase[:, t]))
                    for k in (2 * n, 2 * n + 1):
                        G.indirect_dma_start(out=xs_d, out_offset=bass.IndirectOffsetOnAxis(ap=slot[:, k:k + 1], axis=0),
                                             in_=xn[:, k, :], in_offset=None).then_inc(sm("scattered"), 16)

        def attention_act(act, L):
            for b, s in steps:
                if ok(b):
                    n = 8 * b + s
                    if n >= 4:
                        act.wait_ge(*upto("pv_done", L, (n - 4) // 2 + 1))
                    for r in range(2):
                        u = 2 * n + r
                        act.wait_ge(*upto("st_done", L, u + 1))
                        C.activation(ex[:, n % 4, r, :, :], st_bank[u % 3][:, :].rearrange("p (k q) -> p k q", k=2), ACT.Exp, scale=ISQ).then_inc(sm("exp_done"), 1)
                n = transposed_at(b, s)
                if n is not None:
                    act.wait_ge(*upto("t_done", L, n + 1))
                    if L == 0:
                        if n >= 2:
                            act.wait_ge(*upto("parts_ready", L, n - 1))
                            act.wait_ge(*upto("q_loaded", L, 16 * SLOTS * ((n - 2) // RING + 1), (n - 2) % RING))
                        C.copy(qf[:, n % 2, :], misc[:, 0:S]).then_inc(sm("q_evac"), 1)
                        C.copy(qparts[:, n % 2, 0, :], misc[:, 0:S]).then_inc(sm("q_evac"), 1)
                    else:
                        C.copy(xnt[:, :], misc[:, 0:S]).then_inc(sm("xnt_evac"), 1)
                n = queries_at(b, s)
                if L == 1 and n is not None:
                    act.wait_ge(sm("qp_done"), n + 1)
                    if n >= 2:
                        act.wait_ge(*upto("parts_ready", L, n - 1))
                        act.wait_ge(*upto("q_loaded", L, 16 * SLOTS * ((n - 2) // RING + 1), (n - 2) % RING))
                    C.activation(qf[:, n % 2, :], misc[:, 0:S], ACT.Identity, bias=bqk[:, 0:1]).then_inc(sm("q_evac"), 1)
                    C.activation(qparts[:, n % 2, 0, :], misc[:, 0:S], ACT.Identity, bias=bqk[:, 0:1]).then_inc(sm("q_evac"), 1)
                if L == 0 and (b, s) == (-3, 6):
                    keys0_chunks_act(act, (2, 3))
                if L == 0 and s == 0 and ok(b - 3):
                    act.wait_ge(sm("t2_done"), b - 2)
                    C.copy(t2[:, :], misc[:, 0:S]).then_inc(sm("t2_evac"), 1)
                if L == 0 and s == 1 and ok(b - 3):
                    n = b - 3
                    act.wait_ge(sm("lg_done"), n + 1)
                    C.copy(lg[:, 2 * n:2 * n + 2, :], misc[:, 0:2 * E8].rearrange("p (t e) -> p t e", t=2)).then_inc(sm("lg_evac"), 1)
                if s == 1 and ok(b - 1):
                    act.wait_ge(*upto("pv_done", L, 4 * b))
                    if b >= 2:
                        act.wait_ge(*upto("ott_done", L, b - 1))
                    C.copy(ot[:, :, :], o_bank[:, :].rearrange("p (a q) -> p a q", a=2)).then_inc(sm("ot_evac"), 1)
                if s == 3 and ok(b - 1):
                    act.wait_ge(*upto("ont_done", L, b))
                    C.copy(ont[:, :], misc[:, 0:S]).then_inc(sm("ont_evac"), 1)
                if s == 5 and ok(b + 1):
                    n = b + 1
                    act.wait_ge(*upto("mt_done", L, n + 1))
                    if n >= 2:
                        act.wait_ge(*upto("m_loaded", L, 16 * (n // 2), n % 2))
                    if L == 0 and n == 0:
                        act.wait_ge(sm("neg_stored"), 16 * 2)
                    C.copy(mt[:, n % 2, :], misc[0:48, 0:S]).then_inc(sm("mt_evac"), 1)

        ln_steps = [0]

        def ln_dve(dve, L, b, u):
            c0, c1 = ln_cols(b)
            c = slice(c0, c1)
            ve, y, a, hv = (nw[:, b % 2, i, c] for i in range(4))
            if u >= LN_LEN:
                return
            if ln_steps[0]:
                dve.wait_ge(sm("ln_step"), ln_steps[0])
            ln_steps[0] += 1
            if u == 0:
                for i in range(c0, c1):
                    t = 2 * (b + 4) + i if i < 2 else 2 * (b - 2) + i - 2
                    if i == 0 and L == 0:
                        dve.wait_ge(sm("ld_x", 0 if b + 4 < 2 else 1), 16)
                    if i == 2:
                        dve.wait_ge(*upto("x_done", L, b - 1))
                    if i == 0 and L == 1:
                        dve.wait_ge(sm("combined"), b + 5)
                    last = V.bn_stats(stat[:, b % 2, i, :], x[:, t, :])
            elif u == 1:
                for i in range(c0, c1):
                    last = V.bn_aggr(mv[:, b % 2, i, :], stat[:, b % 2, i, :])
            elif u == 2:
                last = V.tensor_scalar(ve, mv[:, b % 2, c, 1], EPS, None, ALU.add)
            elif u == 3:
                V.tensor_scalar(hv, ve, -0.5, None, ALU.mult)
                last = V.tensor_scalar(a.bitcast(I32), ve.bitcast(I32), 1, None, ALU.logical_shift_right)
            elif u == 4:
                if ok(b + 2):
                    dve.wait_ge(*upto("xn_ready", L, b + 3))
                if ok(b - 4):
                    dve.wait_ge(*upto("xn2_ready", L, b - 3))
                last = V.tensor_scalar(y.bitcast(I32), a.bitcast(I32), -1.0, float(0x5F3759DF), ALU.mult, ALU.add)
            elif u < LN_LEN - 1:
                if u % 3 == 2:
                    last = V.tensor_tensor(a, y, y, ALU.mult)
                elif u % 3 == 0:
                    last = V.tensor_tensor(a, a, hv, ALU.mult)
                else:
                    last = V.scalar_tensor_tensor(y, a, 1.5, y, ALU.add, ALU.mult)
            else:
                last = V.scalar_tensor_tensor(nmr[:, b % 2, c], mv[:, b % 2, c, 0], -1.0, y, ALU.mult, ALU.mult)
            last.then_inc(sm("ln_step"), 1)

        def heads_dve(dve, L, b):
            def dl(ins):
                link(dve, ins, "dve_chain")
            dve.wait_ge(*upto("ott_done", L, b))
            if b >= 2:
                dve.wait_ge(*upto("ont_done", L, b - 1))
            q4 = misc[:, :].rearrange("q (t a j c) -> q t a j c", t=2, a=2, j=4)
            den_a = [q4[:, t, 0, :, 0:27].rearrange("q j (r c) -> q j r c", c=9) for t in range(2)]
            dl(V.reciprocal(rec[:, :, :], misc[:, :].rearrange("q (g c) -> q g c", c=32)[:, :, 0:27].rearrange("q g (r c) -> q g r c", c=9)[:, :, :, DK]))
            for t in range(2):
                V.tensor_tensor(on[:, t, 0:96].rearrange("q (r j d) -> q j r d", j=4, d=DK), den_a[t][:, :, :, 0:DK],
                                rec[:, 8 * t:8 * t + 4, :].unsqueeze(3).to_broadcast([P, 4, 3, DK]), ALU.mult)
                last = V.tensor_tensor(on[:, t, 96:128].rearrange("q (j d) -> q j d", d=DK), q4[:, t, 1, :, 0:DK],
                                       rec[:, 8 * t + 4:8 * t + 8, 0].unsqueeze(2).to_broadcast([P, 4, DK]), ALU.mult)
            last.then_inc(sm("norm_done"), 1)

        def attention_dve(dve, L):
            def dl(ins):
                link(dve, ins, "dve_chain")
            for b, s in steps:
                n, p = scores_at(b, s)
                if L == 1 and s == 7 and ok(b + 5):
                    m = b + 5
                    dve.wait_ge(sm("gathered", m), 32)
                    for t in (2 * m, 2 * m + 1):
                        last = V.scalar_tensor_tensor(x[:, t, :], ctxt[:, t, :], gate[:, t:t + 1], x[:, t, :], ALU.mult, ALU.add)
                    last.then_inc(sm("combined"), 1)
                for r in range(2):
                    if ok(n):
                        u = 16 * n + 2 * p + r
                        dve.wait_ge(*upto("a_done", L, u + 1))
                        if n >= 2:
                            dve.wait_ge(*upto("mx_ready", L, n - 1))
                        V.reduce_max(mx[:, n % 2, :, r, p], a_bank[u % 3][:, :].rearrange("q (t k) -> q t k", t=2), AX.X).then_inc(sm("red_done"), 1)
                    if ok(b + 4) or ok(b - 2):
                        ln_dve(dve, L, b, 2 * s + r)
                    if (s, r) == (2, 0) and ok(b - 1):
                        heads_dve(dve, L, b)
                n = parts_at(b, s)
                if n is not None and b < 0:
                    dve.wait_ge(*upto("q_evac", L, 2 * n + 2))
                    if n >= 2:
                        dve.wait_ge(*upto("q_loaded", L, 16 * SLOTS * ((n - 2) // RING + 1), (n - 2) % RING))
                    dl(V.tensor_tensor(qr[:, :], qf[:, n % 2, :], qparts[:, n % 2, 0, :], ALU.subtract))
                    dl(V.tensor_copy(qparts[:, n % 2, 1, :], qr[:, :]))
                    V.tensor_tensor(qparts[:, n % 2, 2, :], qr[:, :], qparts[:, n % 2, 1, :], ALU.subtract).then_inc(sm("parts_ready"), 1)
                if L == 0 and (b, s) == (-4, 7):
                    keys0_dve(dve, 0)
                if L == 0 and (b, s) == (-3, 5):
                    cperm_dve(dve, range(8, NT))
                if L == 0 and (b, s) in ((-3, 6), (-3, 7), (-2, 0)):
                    keys0_dve(dve, 8 * b + s + 24 - 5)
                if L == 0 and s == 1 and ok(b - 3):
                    m = b - 3
                    dve.wait_ge(sm("lg_evac"), m + 1)
                    for t in (2 * m, 2 * m + 1):
                        last = V.max(v8[:, t, :], lg[:, t, :])
                    last.then_inc(sm("top"), 1)
                if L == 0 and s in (2, 3, 4) and ok(b - 3):
                    m = b - 3
                    tt = slice(2 * m, 2 * m + 2)
                    if s == 2:
                        dve.wait_ge(sm("top"), m + 1)
                        if m == 0:
                            dve.wait_ge(sm("consts"), 7)
                        dl(V.tensor_tensor(tmp[:, tt, :], lg[:, tt, :], v8[:, tt, 0:1].to_broadcast([P, 2, E8]), ALU.is_equal))
                        V.tensor_tensor(tmp[:, tt, :], tmp[:, tt, :], epri[:, :].unsqueeze(1).to_broadcast([P, 2, E8]), ALU.mult).then_inc(sm("pri"), 1)
                    elif s == 3:
                        dve.wait_ge(sm("pri"), m + 1)
                        V.reduce_max(m1[:, tt], tmp[:, tt, :], AX.X).then_inc(sm("first"), 1)
                    else:
                        dve.wait_ge(sm("first"), m + 1)
                        V.tensor_tensor(oh[:, tt, :], tmp[:, tt, :], m1[:, tt].unsqueeze(2).to_broadcast([P, 2, E8]), ALU.is_equal).then_inc(sm("oh_done"), 1)
                if L == 0 and s == 7 and ok(b - 3):
                    m = b - 3
                    tt = slice(2 * m, 2 * m + 2)
                    dve.wait_ge(sm("pos_done"), m + 1)
                    V.tensor_tensor(tmp[:, tt, :], misc[:, 0:2 * E8].rearrange("p (t e) -> p t e", t=2), oh[:, tt, :], ALU.mult).then_inc(sm("pos_evac"), 1)
                    if m == B - 1:
                        V.tensor_copy(cnt[:, :], misc[:, 2 * E8:3 * E8]).then_inc(sm("pos_evac"), 1)
                if L == 0 and s == 0 and ok(b - 4):
                    m = b - 4
                    tt = slice(2 * m, 2 * m + 2)
                    dve.wait_ge(sm("pos_evac"), m + 1)
                    V.reduce_sum(posf[:, tt], tmp[:, tt, :], AX.X).then_inc(sm("pos_red"), 1)
                if L == 1 and s == 0 and ok(b - 3):
                    m = b - 3
                    dve.wait_ge(*upto("xn2_ready", 1, m + 1))
                    V.reduce_max(am[:, 4, m:m + 1], flat(xn[:, 2 * m:2 * m + 2, :]), AX.X, apply_absolute_value=True).then_inc(sm("x_amax"), 1)
                if s == 4 and ok(b - 1):
                    dve.wait_ge(*upto("y_done", L, b))
                    dve.wait_ge(*upto("bias_added", L, b))
                    xx = x[:, 2 * b - 2:2 * b, :]
                    V.tensor_tensor(xx, misc[:, 0:S].rearrange("p (t d) -> p t d", t=2), xx, ALU.add).then_inc(sm("x_done"), 1)

        def attention_pe(pe, L):
            free = []

            def take():
                for s_, v in free:
                    pe.wait_ge(s_, v)
                free.clear()

            for b, s in steps:
                if ok(b):
                    n = 8 * b + s
                    if s == 0:
                        pe.wait_ge(*upto("m_loaded", L, 16 * (b // 2 + 1), b % 2))
                    for r in range(2):
                        u = 2 * n + r
                        if u >= 3:
                            pe.wait_ge(*upto("exp_done", L, u - 2))
                        for t in range(TPB):
                            last = T.matmul(st_bank[u % 3][:, S * t:S * t + S], kstack[:, b % RING, r, s, P * t:P * t + P],
                                            qstack[:, b % RING, s, :], start=(t == 0), stop=(t == 1), skip_group_check=True)
                        last.then_inc(sm("st_done"), 1)
                n, p = scores_at(b, s)
                if ok(n):
                    if p == 0:
                        pe.wait_ge(*upto("q_loaded", L, 16 * SLOTS * (n // RING + 1), n % RING))
                        if L == 0 and n == 0:
                            pe.wait_ge(sm("k_first"), 32)
                        elif L == 0:
                            pe.wait_ge(sm(f"k_loaded{L}", n % RING), 32 * (n // RING + (n % RING > 0)))
                        else:
                            pe.wait_ge(sm(f"k_loaded{L}", n % RING), 32 * (n // RING + 1))
                    for r in range(2):
                        u = 16 * n + 2 * p + r
                        if u >= 3:
                            pe.wait_ge(*upto("red_done", L, u - 2))
                        if u == 2:
                            pe.wait_ge(sm("d_k", 0) if L == 0 else sm("d_v1"), 4)
                        for t in range(TPB):
                            last = T.matmul(a_bank[u % 3][:, S * t:S * t + S], qstack[0:MROW, n % RING, p, P * t:P * t + P],
                                            kstack[0:MROW, n % RING, r, p, :], start=(t == 0), stop=(t == 1), skip_group_check=True)
                        last.then_inc(sm("a_done"), 1)
                if s == 1 and ok(b - 1) or s in (3, 5, 7) and ok(b):
                    n, q = (b - 1, 3) if s == 1 else (b, (s - 3) // 2)
                    pe.wait_ge(*upto("exp_done", L, 16 * n + 4 * q + 4))
                    if q == 0:
                        pe.wait_ge(*upto("v_ready", L, n + 1))
                        if n >= 1:
                            pe.wait_ge(*upto("ot_evac", L, n))
                    for t in range(TPB):
                        for j in range(4):
                            h = 4 * q + j
                            last = T.matmul(o_bank[32 * j:32 * j + 32, S * (q // 3):S * (q // 3) + S], vpad[:, n % 2, t, h, :],
                                            ex[:, (8 * n + 2 * q + j // 2) % 4, j % 2, t, :],
                                            start=(q in (0, 3) and t == 0), stop=(q in (2, 3) and t == 1), skip_group_check=True)
                    last.then_inc(sm("pv_done"), 1)
                if L == 0 and s == 0 and ok(b - 3):
                    n = b - 3
                    pe.wait_ge(*upto("xn2_ready", 0, n + 1))
                    take()
                    for t in range(TPB):
                        last = T.transpose(misc[:, P * t:P * t + P], xn[:, 2 * n + t, :], ident[:, :])
                    last.then_inc(sm("t2_done"), 1)
                    free.append((sm("t2_evac"), n + 1))
                if L == 0 and s == 1 and ok(b - 3):
                    n = b - 3
                    take()
                    for t in range(TPB):
                        last = T.matmul(misc[:, E8 * t:E8 * t + E8], t2[:, P * t:P * t + P], wr[:, :], start=(t == 0), stop=(t == 1), skip_group_check=True)
                    last.then_inc(sm("lg_done"), 1)
                    free.append((sm("lg_evac"), n + 1))
                if s == 2 and ok(b - 1):
                    pe.wait_ge(*upto("ot_evac", L, b))
                    take()
                    for t in range(TPB):
                        for a in range(2):
                            k = 2 * t + a
                            last = T.transpose(misc[:, P * k:P * k + P], ot[:, a, P * t:P * t + P], ident[:, :])
                    last.then_inc(sm("ott_done"), 1)
                    free.append(upto("norm_done", L, b))
                if s == 3 and ok(b - 1):
                    take()
                    for t in range(TPB):
                        last = T.transpose(misc[:, P * t:P * t + P], on[:, t, :], ident[:, :])
                    last.then_inc(sm("ont_done"), 1)
                    free.append(upto("ont_evac", L, b))
                if s == 4 and ok(b - 1):
                    take()
                    for t in range(TPB):
                        last = T.matmul(misc[:, P * t:P * t + P], ont[:, P * t:P * t + P], wo[L][:, :],
                                        start=(t == 0), stop=(t == 1), skip_group_check=True)
                    last.then_inc(sm("y_done"), 1)
                    free.append(upto("x_done", L, b))
                if s == 5 and ok(b + 1):
                    n = b + 1
                    pe.wait_ge(*upto("mx_ready", L, n + 1))
                    take()
                    for t in range(TPB):
                        last = T.matmul(misc[0:48, P * t:P * t + P], mparts[:, t, :, :, :].rearrange("q r c p -> q (r c p)"), identb[:, :],
                                        start=(t == 0), stop=(t == 1), skip_group_check=True)
                    last.then_inc(sm("mt_done"), 1)
                    free.append(upto("mt_evac", L, n + 1))
                if L == 0 and (b, s) == (-3, 6):
                    keys0_chunks_pe(pe, (2, 3))
                n = transposed_at(b, s)
                if n is not None:
                    pe.wait_ge(*upto("xn_ready", L, n + 1))
                    take()
                    for t in range(TPB):
                        last = T.transpose(misc[:, P * t:P * t + P], xn[:, 2 * n + t, :], ident[:, :])
                    last.then_inc(sm("t_done"), 1)
                    free.append(upto("q_evac", L, 2 * n + 2) if L == 0 else (sm("xnt_evac"), n + 1))
                n = queries_at(b, s)
                if L == 1 and n is not None:
                    take()
                    T.matmul(misc[:, 0:S], wq[:, :], xnt[:, :], start=True, stop=True).then_inc(sm("qp_done"), 1)
                    free.append(upto("q_evac", L, 2 * n + 2))
                if L == 0 and s == 7 and ok(b - 3):
                    n = b - 3
                    pe.wait_ge(sm("run_done"), n + 1)
                    if n == 0:
                        pe.wait_ge(sm("consts"), 7)
                    take()
                    for t in range(TPB):
                        T.matmul(misc[:, E8 * t:E8 * t + E8], before[:, :], oh[:, 2 * n + t, :], start=(t == 0), stop=False, skip_group_check=True)
                        last = T.matmul(misc[:, E8 * t:E8 * t + E8], ones[:, :], run[:, 2 * n + t, :], start=False, stop=(t == 1), skip_group_check=True)
                    if n == B - 1:
                        last = T.matmul(misc[:, 2 * E8:3 * E8], ones[:, :], run[:, NT, :], start=False, stop=True, skip_group_check=True)
                    last.then_inc(sm("pos_done"), 1)
                    free.append((sm("pos_evac"), n + 1 if n < B - 1 else B + 1))
            take()

        t_bank, h_bank, y_bank = ps[4], [ps[5], ps[6]], ps[7]

        def wbuf(i):
            return ex_flat[:, 2 * HID * (i % 4):2 * HID * (i % 4) + 2 * HID]

        def experts_sp(sp):
            sp.wait_ge(sm("consts"), 7)
            sp.dma_start(xs_d[E8 * REG:E8 * REG + P, :], zt[:, :]).then_inc(sm("xs_zeroed"), 16)
            sp.wait_ge(sm("cnt_ready"), 1)
            for e in range(5):
                c = sp.value_load(cnt_i[0:1, e:e + 1], min_val=0, max_val=B * S)
                sp.dma_start(xs_d[bass.ds(c + e * REG, P), :], zt[:, :]).then_inc(sm("xs_zeroed"), 16)
            sp.wait_ge(sm("xs_zeroed"), 16 * (E8 + 1))
            sp.wait_ge(sm("scattered"), 16 * NT)
            sp.wait_ge(sm("tab_ready"), 1)
            for i in range(MT + 5):
                if i < MT:
                    r = sp.value_load(tbase[0:1, i:i + 1], min_val=0, max_val=E8 * REG)
                    if i >= 4:
                        sp.wait_ge(sm("st_done2"), i - 3)
                    sp.dma_start(xsb[:, i % 4, :], xs_d[bass.ds(r, P), :]).then_inc(sm("xs_loaded", i % 4), 16)
                if 12 <= i < 12 + SLOTS:
                    keys_slot_sp(sp, 1, i - 12, slice(0, B * S), "kd_stored")
                if i >= 5:
                    k = i - 5
                    sp.wait_ge(sm("ye_evac"), k + 1)
                    sp.dma_start(ys_d[k * P:k * P + P, :], ysb[:, k % 2, :]).then_inc(sm("y_stored", k % 2), 16)

        def experts_pool(pool):
            for c in range(4):
                col = slice(512 * c, 512 * c + 512)
                pool.wait_ge(sm("a_k", 1), 2 * c + 2)
                link(pool, G.tensor_tensor(kr[:, col], kr[:, col], kp[:, 0, col], ALU.subtract), "pool_chain")
                link(pool, G.tensor_copy(kp[:, 1, col], kr[:, col]), "pool_chain")
                G.tensor_tensor(kp[:, 2, col], kr[:, col], kp[:, 1, col], ALU.subtract).then_inc(sm("d_k", 1), 1)
            pool.wait_ge(sm("y_stored", 0), 16 * ((MT + 1) // 2))
            pool.wait_ge(sm("y_stored", 1), 16 * (MT // 2))
            pool.wait_ge(sm("tab_ready"), 1)

        def experts_act(act):
            act.wait_ge(sm("gdiff"), 1)
            C.activation(gate[:, :], gate[:, :], ACT.Exp).then_inc(sm("gexp"), 1)
            C.activation(spare[:, :], bqk[:, 0:1], ACT.Gelu)
            act.wait_ge(sm("consts"), 7)
            act.wait_ge(sm("cnt_ready"), 1)
            for e in range(5, E8):
                c = act.value_load(cnt_i[0:1, e:e + 1], min_val=0, max_val=B * S)
                act.dma_start(xs_d[bass.ds(c + e * REG, P), :], zt[:, :]).then_inc(sm("xs_zeroed"), 16)
            keys1_act(act)
            for i in range(-1, MT):
                if i + 1 < MT:
                    k = i + 1
                    act.wait_ge(sm("st_done2"), k + 1)
                    if k >= 2:
                        act.wait_ge(sm("h_done"), k - 1)
                    C.copy(xst[:, k % 2, :], t_bank[:, 0:P]).then_inc(sm("st_evac2"), 1)
                if i >= 0:
                    act.wait_ge(sm("h_done"), i + 1)
                    if i >= 2:
                        act.wait_ge(sm("ye_done"), i - 1)
                    C.activation(hg[:, i % 2, :], h_bank[i % 2][:, :], ACT.Gelu).then_inc(sm("g_done"), 1)
                if i == 16:
                    for k in range(3):
                        act.wait_ge(sm("wt_done"), k + 1)
                        C.copy(w3t[:, FF * k:FF * k + FF], ps[k][:, 0:FF]).then_inc(sm("wt_evac"), 1)

        def tables_dve(dve):
            def dl(ins):
                link(dve, ins, "dve_chain")
            dve.wait_ge(sm("pos_evac"), B + 1)
            V.tensor_copy(cnt_i[:, :], cnt[:, :]).then_inc(sm("cnt_ready"), 1)
            V.tensor_tensor(gate[:, :], v8[:, :, 1], v8[:, :, 0], ALU.subtract).then_inc(sm("gdiff"), 1)
            dl(V.tensor_scalar(ntile_i[:, :], cnt[:, :], 1.0 / P, 0.5 - 0.5 / P, ALU.mult, ALU.add))
            dl(V.tensor_copy(ntile[:, :], ntile_i[:, :]))
            dl(V.tensor_copy(incl[:, :], ntile[:, :]))
            for e in range(1, E8):
                dl(V.tensor_tensor(incl[:, e:e + 1], incl[:, e - 1:e], ntile[:, e:e + 1], ALU.add))
            dl(V.tensor_tensor(cmp_[:, :, :], incl[:, :].unsqueeze(1).to_broadcast([P, MT, E8]), tidx[:, :].unsqueeze(2).to_broadcast([P, MT, E8]), ALU.is_le))
            V.reduce_sum(texpf[:, :], cmp_[:, :, :], AX.X).then_inc(sm("texpf"), 1)
            dve.wait_ge(sm("texpf"), 1)
            dl(V.tensor_tensor(cmp_[:, :, :], cmp_[:, :, :], ntile[:, :].unsqueeze(1).to_broadcast([P, MT, E8]), ALU.mult))
            dl(V.reduce_sum(toff[:, :], cmp_[:, :, :], AX.X))
            dl(V.tensor_tensor(toff[:, :], tidx[:, :], toff[:, :], ALU.subtract))
            dl(V.tensor_scalar(toff[:, :], toff[:, :], float(P), None, ALU.mult))
            dl(V.scalar_tensor_tensor(toff[:, :], texpf[:, :], float(REG), toff[:, :], ALU.mult, ALU.add))
            dl(V.tensor_scalar(tbase[:, :], toff[:, :], float(E8 * REG), None, ALU.min))
            dl(V.tensor_scalar(texp[:, :], texpf[:, :], float(E8 - 1), None, ALU.min))
            dl(V.tensor_tensor(excl[:, :], incl[:, :], ntile[:, :], ALU.subtract))
            dl(V.tensor_scalar(excl[:, :], excl[:, :], float(P), None, ALU.mult))
            dve.wait_ge(sm("pos_red"), B)
            dl(V.tensor_tensor(tmp[:, :, :], oh[:, :, :], excl[:, :].unsqueeze(1).to_broadcast([P, NT, E8]), ALU.mult))
            dl(V.reduce_sum(texpf[:, 0:NT], tmp[:, :, :], AX.X))
            V.tensor_tensor(gslot[:, :], posf[:, :], texpf[:, 0:NT], ALU.add).then_inc(sm("tab_ready"), 1)

        def experts_dve(dve):
            def dl(ins):
                link(dve, ins, "dve_chain")
            tables_dve(dve)
            dve.wait_ge(sm("gexp"), 1)
            dl(V.tensor_scalar(gate[:, :], gate[:, :], 1.0, None, ALU.add))
            dl(V.reciprocal(gate[:, :], gate[:, :]))
            dve.wait_ge(sm("ld_e"), 16 * (2 * E8 + 2))
            dve.wait_ge(*upto("pv_done", 0, 4 * B))
            for i in range(MT + 2):
                if i < MT:
                    if i >= 4:
                        dve.wait_ge(sm("ye_done"), i - 3)
                    e = dve.value_load(texp[0:1, i:i + 1], min_val=0, max_val=E8 - 1)
                    V.tensor_copy(wbuf(i), w12[:, bass.ds(e * (2 * HID), 2 * HID)]).then_inc(sm("w_copied"), 1)
                if 5 <= i < 9:
                    values1_dve(dve, i - 5)
                wb = w3[:, :].rearrange("p (n k) -> p n k", k=BLK)
                n3 = 3 * FF // BLK
                if i == 9:
                    dve.wait_ge(sm("ld_w"), 16 * 12)
                    dl(V.reduce_max(wam[:, :], wb, AX.X, apply_absolute_value=True))
                if i == 10:
                    dl(V.tensor_scalar(wam[:, :], wam[:, :], 1.0 / W_QMAX, TINY, ALU.mult, ALU.max))
                    dl(V.reciprocal(wrs[:, :], wam[:, :]))
                if i == 11:
                    dl(V.tensor_tensor(w3i[:, :].rearrange("p (n k) -> p n k", k=BLK), wb, wrs[:, :].unsqueeze(2).to_broadcast([P, n3, BLK]), ALU.mult))
                if i == 12:
                    V.tensor_tensor(wb, w3i[:, :].rearrange("p (n k) -> p n k", k=BLK), wam[:, :].unsqueeze(2).to_broadcast([P, n3, BLK]), ALU.mult).then_inc(sm("wq_done"), 1)
                if i >= 2:
                    k = i - 2
                    dve.wait_ge(sm("ye_done"), k + 1)
                    if k >= 2:
                        dve.wait_ge(sm("y_stored", k % 2), 16 * (k // 2))
                    V.tensor_copy(ysb[:, k % 2, :], y_bank[:, 0:P]).then_inc(sm("ye_evac"), 1)

        def experts_pe(pe):
            keys1_pe(pe)
            pe.wait_ge(*upto("red_done", 0, 16 * B))
            pe.wait_ge(*upto("ot_evac", 0, B))
            for i in range(-1, MT + 1):
                if i + 1 < MT:
                    k = i + 1
                    pe.wait_ge(sm("xs_loaded", k % 4), 16 * (k // 4 + 1))
                    if k >= 1:
                        pe.wait_ge(sm("st_evac2"), k)
                    T.transpose(t_bank[:, 0:P], xsb[:, k % 4, :], ident[:, :]).then_inc(sm("st_done2"), 1)
                if 0 <= i < MT:
                    pe.wait_ge(sm("st_evac2"), i + 1)
                    pe.wait_ge(sm("w_copied"), i + 1)
                    if i >= 2:
                        pe.wait_ge(sm("g_done"), i - 1)
                    for c in range(HC):
                        last = T.matmul(h_bank[i % 2][:, P * c:P * c + P], wbuf(i)[:, P * c:P * c + P], xst[:, i % 2, :],
                                        start=(c == 0), stop=(c == HC - 1), skip_group_check=True)
                    last.then_inc(sm("h_done"), 1)
                if i >= 1:
                    k = i - 1
                    pe.wait_ge(sm("g_done"), k + 1)
                    if k >= 1:
                        pe.wait_ge(sm("ye_evac"), k)
                    for c in range(HC):
                        last = T.matmul(y_bank[:, 0:P], hg[:, k % 2, P * c:P * c + P], wbuf(k)[:, HID + P * c:HID + P * c + P],
                                        start=(c == 0), stop=(c == HC - 1))
                    last.then_inc(sm("ye_done"), 1)
                if 4 <= i < 8:
                    values1_pe(pe, i - 4)
                if i == 15:
                    pe.wait_ge(sm("wq_done"), 1)
                    pe.wait_ge(sm("d_v1"), 3)
                    for k in range(3):
                        for c in range(FC):
                            last = T.transpose(ps[k][:, P * c:P * c + P], w3[:, FF * k + P * c:FF * k + P * c + P], ident[:, :])
                        last.then_inc(sm("wt_done"), 1)

        xit = c28[:, 0:2048]
        gi = w12[:, 0:3072].bitcast(I16)
        ui = w12[:, 3072:6144].bitcast(I16)
        sig = [w12[:, 6144 + 512 * i:6656 + 512 * i] for i in range(4)]
        sq = [c28[:, 2048 + 256 * i:2304 + 256 * i].bitcast(U16) for i in range(4)]
        u_blocks = [kst_f[:, 512 * i:512 * i + 512] for i in range(NB, 16)] + [qst_f[:, 512 * i:512 * i + 512] for i in range(8)]

        def gb(i):
            return kst_f[:, 512 * i:512 * i + 512]

        def ub(i):
            return u_blocks[i]

        def gib(i):
            return gi[:, 512 * i:512 * i + 512]

        def uib(i):
            return ui[:, 512 * i:512 * i + 512]

        def col(i):
            return sc[:, i:i + 1]

        def ff_sp(sp):
            o_v = out.rearrange("b (t p) d -> p (b t) d", p=P)
            for c in range(4):
                sp.wait_ge(sm("out_ready"), c + 1)
                sp.dma_start(o_v[:, 4 * c:4 * c + 4, :], x[:, 4 * c:4 * c + 4, :]).then_inc(sm("stored"), 16)
            sp.wait_ge(sm("stored"), 64)

        def ff_pool(pool):
            def gmax(k):
                pool.wait_ge(sm("max_own"), k + 1)
                G.partition_all_reduce(col(k + 8), col(k), P, bass.bass_isa.ReduceOp.max).then_inc(sm("max_all"), 1)
            gmax(0)
            gmax(1)
            gmax(2)
            gmax(3)
            gmax(4)

        def ff_act(act):
            C.activation(spare[:, :], bqk[:, 0:1], ACT.Sigmoid)
            for c in range(4):
                act.wait_ge(sm("xt_done"), c + 1)
                C.activation(xit[:, 512 * c:512 * c + 512], ps[4 + c][:, :], ACT.Copy, bias=-MAGIC).then_inc(sm("xt_evac"), 1)

            def evac(i):
                act.wait_ge(sm("gu_done"), i + 1)
                C.copy(gb(i) if i < NB else ub(i - NB), ps[i % 4][:, :]).then_inc(sm("gu_evac"), 1)
            for i in range(NB + 2):
                evac(i)
            act.wait_ge(sm("scales"), 1)
            for i in range(NB + 2):
                if i < NB:
                    C.activation(gib(i), gb(i), ACT.Copy, scale=col(17)).then_inc(sm("gi_done"), 1)
                if 1 <= i <= NB:
                    act.wait_ge(sm("gi_done"), i)
                    if i >= 5:
                        act.wait_ge(sm("sq_done"), (i - 5) // 2 + 1 if i % 2 else (i - 4) // 2)
                        act.wait_ge(sm("sq_act"), (i - 4) // 2)
                    C.activation(sig[(i - 1) % 4], gib(i - 1), ACT.Sigmoid, scale=col(16)).then_inc(sm("sg_done"), 1)
                if i >= 2 and i % 2:
                    act.wait_ge(sm("sg_done"), i - 1)
                    if i >= 6:
                        act.wait_ge(sm("p_done"), i - 5)
                    C.activation(sq[(i - 2) % 4], sig[(i - 2) % 4], ACT.Copy, scale=65536.0).then_inc(sm("sq_act"), 1)
                if i < 5:
                    evac(NB + 2 + 2 * i)
                    evac(NB + 3 + 2 * i)
            for i in range(5):
                up_int(act, i)
            act.wait_ge(sm("scales"), 3)
            act.wait_ge(sm("p_done"), NB)
            for i in range(NB):
                C.activation(gib(i), gb(i), ACT.Copy, scale=col(21)).then_inc(sm("ai_done"), 1)
                if 5 + i < NB:
                    up_int(act, 5 + i)
            for i in range(NB):
                act.wait_ge(sm("o_magic"), i + 1)
                C.activation(gb(i), gb(i), ACT.Copy, bias=-MAGIC).then_inc(sm("o_int"), 1)

        def up_int(act, i):
            if i == 0:
                act.wait_ge(sm("scales"), 2)
            C.activation(uib(i), ub(i), ACT.Copy, scale=col(19)).then_inc(sm("ui_done"), 1)

        def ff_dve(dve):
            def dl(ins):
                link(dve, ins, "dve_chain")

            def scale_of(m, true, dst, n):
                dl(V.tensor_tensor(col(m), col(m), col(true), ALU.mult))
                dl(V.tensor_scalar(col(dst), col(m), 1.0 / ACT_QMAX, TINY, ALU.mult, ALU.max))
                dl(V.reciprocal(col(dst + 1), col(dst)))
                V.tensor_tensor(col(dst + 1), col(dst + 1), col(true), ALU.mult).then_inc(sm("scales"), 1)
                dve.wait_ge(sm("scales"), n)

            dve.wait_ge(sm("x_amax"), B)
            V.reduce_max(col(0), am[:, 4, 0:B], AX.X).then_inc(sm("max_own"), 1)
            dve.wait_ge(sm("max_all"), 1)
            dl(V.tensor_scalar(col(14), col(8), 1.0 / ACT_QMAX, TINY, ALU.mult, ALU.max))
            dl(V.reciprocal(col(15), col(14)))
            for t in range(4):
                V.tensor_scalar(xn[:, 4 * t:4 * t + 4, :], xn[:, 4 * t:4 * t + 4, :], col(15), MAGIC, ALU.mult, ALU.add).then_inc(sm("xq_done"), 1)

            def amax(k, i, src):
                return V.reduce_max(am[:, k, i:i + 1], src, AX.X, apply_absolute_value=True)
            for i in range(NB):
                dve.wait_ge(sm("gu_evac"), i + 1)
                last = amax(0, i, gb(i))
            dl(last)
            V.reduce_max(col(1), am[:, 0, 0:NB], AX.X).then_inc(sm("max_own"), 1)
            for i in range(2):
                dve.wait_ge(sm("gu_evac"), NB + i + 1)
                amax(1, i, ub(i))
            dve.wait_ge(sm("max_all"), 2)
            scale_of(9, 14, 16, 1)
            def product(i):
                if i % 2:
                    dve.wait_ge(sm("sq_act"), i // 2 + 1)
                else:
                    dve.wait_ge(sm("sq_done"), i // 2 + 1)
                V.tensor_tensor(gb(i), gib(i), sq[i % 4], ALU.mult).then_inc(sm("p_done"), 1)

            for i in range(NB):
                for j in (2 * i + 2, 2 * i + 3):
                    if j < NB:
                        dve.wait_ge(sm("gu_evac"), NB + j + 1)
                        last = amax(1, j, ub(j))
                if i == 5:
                    dl(last)
                    V.reduce_max(col(2), am[:, 1, 0:NB], AX.X).then_inc(sm("max_own"), 1)
                if i == 7:
                    dve.wait_ge(sm("max_all"), 3)
                    scale_of(10, 14, 18, 2)
                if i % 2 == 0:
                    dve.wait_ge(sm("sg_done"), i + 1)
                    V.tensor_scalar(sq[i % 4], sig[i % 4], 65536.0, None, ALU.mult).then_inc(sm("sq_done"), 1)
                if i >= 1:
                    product(i - 1)
                if i >= 2:
                    dve.wait_ge(sm("p_done"), i - 1)
                    amax(2, i - 2, gb(i - 2))
            product(NB - 1)
            for i in range(NB - 2, NB):
                dve.wait_ge(sm("p_done"), i + 1)
                last = amax(2, i, gb(i))
            dl(last)
            dl(V.tensor_scalar(col(24), col(16), 1.0 / 65536.0, None, ALU.mult))
            V.reduce_max(col(3), am[:, 2, 0:NB], AX.X).then_inc(sm("max_own"), 1)
            dve.wait_ge(sm("max_all"), 4)
            scale_of(11, 24, 20, 3)
            for i in range(NB):
                dve.wait_ge(sm("ai_done"), i + 1)
                dve.wait_ge(sm("ui_done"), i + 1)
                V.tensor_tensor(ub(i), gib(i), uib(i), ALU.mult).then_inc(sm("au_done"), 1)
                if i >= 1:
                    dve.wait_ge(sm("au_done"), i)
                    amax(3, i - 1, ub(i - 1))
            dve.wait_ge(sm("au_done"), NB)
            dl(amax(3, NB - 1, ub(NB - 1)))
            dl(V.tensor_tensor(col(25), col(20), col(18), ALU.mult))
            V.reduce_max(col(4), am[:, 3, 0:NB], AX.X).then_inc(sm("max_own"), 1)
            dve.wait_ge(sm("max_all"), 5)
            scale_of(12, 25, 22, 4)
            for i in range(NB):
                V.tensor_scalar(gb(i), ub(i), col(23), MAGIC, ALU.mult, ALU.add).then_inc(sm("o_magic"), 1)
            for c in range(4):
                down_dve(dve, c)

        def down_dve(dve, c):
            dve.wait_ge(sm("d_done"), c + 1)
            V.scalar_tensor_tensor(x[:, 4 * c:4 * c + 4, :], ps[4 + c][:, :].rearrange("p (t d) -> p t d", t=4), col(22),
                                   x[:, 4 * c:4 * c + 4, :], ALU.mult, ALU.add).then_inc(sm("out_ready"), 1)

        def ff_pe(pe):
            pe.wait_ge(*upto("exp_done", 1, 16 * B))
            pe.wait_ge(*upto("red_done", 1, 16 * B))
            pe.wait_ge(*upto("ot_evac", 1, B))
            for c in range(4):
                pe.wait_ge(sm("xq_done"), c + 1)
                for t in range(4):
                    last = T.transpose(ps[4 + c][:, P * t:P * t + P], xn[:, 4 * c + t, :], ident[:, :])
                last.then_inc(sm("xt_done"), 1)
            pe.wait_ge(sm("wt_evac"), 3)
            for i in range(2 * NB):
                k, j = i // NB, i % NB
                n, c = j // FC, j % FC
                pe.wait_ge(sm("xt_evac"), n + 1 if i < NB else 4)
                if i >= 4:
                    pe.wait_ge(sm("gu_evac"), i - 3)
                T.matmul(ps[i % 4][:, :], w3t[:, FF * k + P * c:FF * k + P * c + P], xit[:, 512 * n:512 * n + 512], start=True, stop=True).then_inc(sm("gu_done"), 1)
            for c in range(4):
                for f in range(FC):
                    pe.wait_ge(sm("o_int"), FC * c + f + 1)
                    for t in range(4):
                        k = P * t
                        last = T.matmul(ps[4 + c][:, P * t:P * t + P], gb(FC * c + f)[:, k:k + P], w3t[:, 2 * FF + P * f:2 * FF + P * f + P],
                                        start=(f == 0 and t == 0), stop=(f == FC - 1 and t == 3), skip_group_check=True)
                last.then_inc(sm("d_done"), 1)

        with nc.Block() as block:
            @block.sync
            def _(sp):
                prologue_sp(sp)
                attention_sp(sp, 0)
                experts_sp(sp)
                attention_sp(sp, 1)
                ff_sp(sp)

            @block.gpsimd
            def _(pool):
                prologue_pool(pool)
                attention_pool(pool, 0)
                experts_pool(pool)
                attention_pool(pool, 1)
                ff_pool(pool)

            @block.scalar
            def _(act):
                prologue_act(act)
                attention_act(act, 0)
                experts_act(act)
                attention_act(act, 1)
                ff_act(act)

            @block.vector
            def _(dve):
                prologue_dve(dve)
                attention_dve(dve, 0)
                experts_dve(dve)
                attention_dve(dve, 1)
                ff_dve(dve)

            @block.tensor
            def _(pe):
                keys0_pe(pe)
                attention_pe(pe, 0)
                experts_pe(pe)
                attention_pe(pe, 1)
                ff_pe(pe)


_INS = ["x", "ctx_1024", "L0_xattn_w_out", "L0_xattn_b_out", "L0_ffn_Wr", "L0_ffn_W1", "L0_ffn_W2", "L1_xattn_W_Q", "L1_xattn_b_Q",
        "L1_xattn_W_K", "L1_xattn_b_K", "L1_xattn_W_V", "L1_xattn_b_V", "L1_xattn_W_O", "L1_xattn_b_O", "L1_ffn_w_gate",
        "L1_ffn_w_up", "L1_ffn_w_down"]


def kernel(**inputs):
    import numpy as _np
    import concourse.bacc as _bacc
    from concourse import mybir as _mybir
    from concourse.bass_utils import run_bass_kernel_spmd as _run

    nc = _bacc.Bacc("TRN2", target_bir_lowering=False, num_devices=1)
    arrays, aps = {}, {}
    laid = {n: _np.ascontiguousarray(inputs[n]) for n in _INS}
    laid["w_out_t"] = _np.ascontiguousarray(_np.asarray(laid.pop("L0_xattn_w_out")).T)
    order = _np.arange(D).reshape(PAIRS, 2, DK).transpose(2, 1, 0).reshape(-1)
    laid["w_q"] = _np.ascontiguousarray(laid.pop("L1_xattn_W_Q")[:, order])
    laid["w_k"] = _np.ascontiguousarray(laid.pop("L1_xattn_W_K")[:, order])
    laid["b_q"] = _np.ascontiguousarray(laid.pop("L1_xattn_b_Q")[order])
    laid["b_k"] = _np.ascontiguousarray(laid.pop("L1_xattn_b_K")[order])
    for name, a in laid.items():
        arrays[f"in_{name}"] = a
        aps[name] = nc.dram_tensor(f"in_{name}", a.shape, _mybir.dt.from_np(a.dtype), kind="ExternalInput").ap()
    out = nc.dram_tensor("out_0", (B, S, D), F32, kind="ExternalOutput").ap()
    emit(nc, aps, out)
    r = _run(nc, [arrays], core_ids=[0])
    return r.results[0]["out_0"]
```
